# Optimizing a Trainium2 kernel written in Bass

```python
import numpy as np
import jax
import jax.numpy as jnp

def _softmax(x, axis=-1):
    return jax.nn.softmax(x, axis=axis)

def _gelu(x):
    return jax.nn.gelu(x, approximate=True)

def _silu(x):
    return jax.nn.silu(x)

def _sigmoid(x):
    return jax.nn.sigmoid(x)

def _layernorm(x, axis=-1, eps=1e-05):
    m = jnp.mean(x, axis=axis, keepdims=True)
    v = jnp.var(x, axis=axis, keepdims=True)
    return (x - m) / jnp.sqrt(v + eps)

def _scatter_add(tgt, idx, src, axis=0):
    return tgt.at[idx].add(src)

def _segment_sum(src, seg, n):
    return jax.ops.segment_sum(src, seg, n)
kernel_name = 'mk_gnn_ffn_d1_gnn_r8_6d8924'

def setup_inputs(seed: int=0):
    np.random.seed(seed)
    _w = jnp.asarray

    def _rec_inputs():
        import jax
        import jax.numpy as jnp
        _gk = jax.random.key(seed)
        x = -0.0003713 + 1 * jax.random.normal(jax.random.fold_in(_gk, 1), (6250, 256), jnp.float32)
        src = jax.random.randint(jax.random.fold_in(_gk, 2), (200000,), 0, 6250, jnp.int32)
        dst = jax.random.randint(jax.random.fold_in(_gk, 3), (200000,), 0, 6250, jnp.int32)
        _o = jnp.argsort(dst, stable=True)
        src = src[_o]
        dst = dst[_o]
        edge_type_8 = jax.random.randint(jax.random.fold_in(_gk, 12), (200000,), 0, 8, jnp.int32)
        return (x, src, dst, edge_type_8)
    x, src, dst, edge_type_8 = _rec_inputs()

    def _L0_gnn_setup():
        import jax, jax.numpy as jnp
        import numpy as np
        N, E, D, R, L = (6250, 31250, 256, 8, 3)
        key = jax.random.key(seed)
        k = jax.random.split(key, 7)
        scale = 1.0 / np.sqrt(D)
        x = jax.random.normal(k[0], (N, D), dtype=jnp.float32)
        edge_index = jax.random.randint(k[1], (2, E), 0, N, dtype=jnp.int64)
        edge_type = jax.random.randint(k[2], (E,), 0, R, dtype=jnp.int64)
        W_rel = jax.random.normal(k[3], (L, R, D, D), dtype=jnp.float32) * scale
        W_root = jax.random.normal(k[4], (L, D, D), dtype=jnp.float32) * scale
        bias = jax.random.normal(k[5], (L, D), dtype=jnp.float32) * 0.02
        return {'x': x, 'edge_index': edge_index, 'edge_type': edge_type, 'W_rel': W_rel, 'W_root': W_root, 'bias': bias}
    _L0_gnn_all = _L0_gnn_setup()
    _L0_gnn_in = {k: v for k, v in _L0_gnn_all.items() if k in ('W_rel', 'W_root', 'bias')}
    del _L0_gnn_all

    def _L0_ffn_setup():
        import jax, jax.numpy as jnp
        import numpy as np
        EPS = 1e-08
        key = jax.random.key(seed)
        kx, kw, kb = jax.random.split(key, 3)
        B, S, K, N = (64, 512, 256, 256)
        x = jax.random.normal(kx, (B, S, K), dtype=jnp.float32)
        bound_w = np.sqrt(6.0 / K) / np.sqrt(1.0 + 5.0)
        weight = jax.random.uniform(kw, (N, K), dtype=jnp.float32, minval=-bound_w, maxval=bound_w)
        bound_b = 1.0 / np.sqrt(K)
        bias = jax.random.uniform(kb, (N,), dtype=jnp.float32, minval=-bound_b, maxval=bound_b)
        return {'x': x, 'weight': weight, 'bias': bias}
    _L0_ffn_all = _L0_ffn_setup()
    _L0_ffn_in = {k: v for k, v in _L0_ffn_all.items() if k in ('weight', 'bias')}
    del _L0_ffn_all
    return {'x': x, 'src': src, 'dst': dst, 'edge_type_8': edge_type_8, 'L0_gnn_W_rel': _L0_gnn_in['W_rel'], 'L0_gnn_W_root': _L0_gnn_in['W_root'], 'L0_gnn_bias': _L0_gnn_in['bias'], 'L0_ffn_weight': _L0_ffn_in['weight'], 'L0_ffn_bias': _L0_ffn_in['bias']}

def reference(x, src, dst, edge_type_8, L0_gnn_W_rel, L0_gnn_W_root, L0_gnn_bias, L0_ffn_weight, L0_ffn_bias):
    import jax
    import jax.numpy as jnp

    def _L0_gnn_ref(x, edge_index, edge_type, W_rel, W_root, bias):
        import jax, jax.numpy as jnp
        import numpy as np
        N, E, D, R, L = (6250, 31250, 256, 8, 3)
        src, dst = (edge_index[0], edge_index[1])
        n_layers = W_rel.shape[0]
        for l in range(n_layers):
            xr = jnp.einsum('nd,rde->rne', x, W_rel[l])
            msg = xr[edge_type, src]
            agg = jax.ops.segment_sum(msg, dst, num_segments=x.shape[0])
            x = jax.nn.relu(agg + x @ W_root[l] + bias[l])
        return x

    def _L0_ffn_ref(x, weight, bias):
        import jax, jax.numpy as jnp
        import numpy as np
        EPS = 1e-08
        'LNS inference path of LNSLinear.\n\n            log_out[m, n] = logsumexp_k(log(|x[m,k]|+eps) + log(|w[n,k]|+eps))\n            out = sign(sign(x) @ sign(w).T) * exp(log_out) + bias\n            Computed stably as log(exp(lx - mx) @ exp(lw - mw).T) + mx + mw.\n            '
        orig_shape = x.shape
        K = weight.shape[1]
        xf = x.reshape(-1, K)
        log_x = jnp.log(jnp.abs(xf) + EPS)
        x_sign = jnp.sign(xf)
        log_w = jnp.log(jnp.abs(weight) + EPS)
        w_sign = jnp.sign(weight)
        mx = jnp.max(log_x, axis=-1, keepdims=True)
        mw = jnp.max(log_w, axis=-1, keepdims=True)
        acc = jnp.einsum('mk,nk->mn', jnp.exp(log_x - mx), jnp.exp(log_w - mw))
        log_out = jnp.log(acc) + mx + mw.T
        out_sign = jnp.sign(jnp.einsum('mk,nk->mn', x_sign, w_sign))
        out = out_sign * jnp.exp(log_out) + bias
        return out.reshape(orig_shape[:-1] + (weight.shape[0],))
    edge_index = jnp.stack([src, dst])
    x = x + _L0_gnn_ref(_layernorm(x, axis=-1), edge_index, edge_type_8, L0_gnn_W_rel, L0_gnn_W_root, L0_gnn_bias)
    x = x + _L0_ffn_ref(_layernorm(x, axis=-1)[None], L0_ffn_weight, L0_ffn_bias)[0]
    return x

_drawn_inputs = setup_inputs


def setup_inputs(seed=0):
    import zlib

    import numpy as np

    out = dict(_drawn_inputs(seed))
    spreads = {}
    factors = {'L0_gnn_bias': 8.0, 'L0_ffn_bias': 200.0}
    for name, (base, spread) in spreads.items():
        noise = np.random.default_rng([zlib.crc32(name.encode()), seed]).standard_normal(out[name].shape)
        drawn = base * np.exp(spread * noise) if base else spread * noise
        out[name] = jnp.asarray(drawn.astype(out[name].dtype))
    for name, factor in factors.items():
        out[name] = (out[name] * factor).astype(out[name].dtype)
    return out
```

```python
from contextlib import ExitStack

import concourse.bass as bass
from concourse import mybir

N, D, E, R, L = 6250, 256, 200000, 8, 3
P = 128
KH = D // P
TILES = -(-N // P)
PAIRS = TILES // 2
LAST_ROWS = N - (TILES - 1) * P
NP_ = TILES * P
CH = 8
GE = CH * P
GROUPS = -(-E // GE)
FULL = E // GE
TAIL = E - FULL * GE
TAIL_P = TAIL // CH
RING = 4
BATCHES = GROUPS // RING
W = 64
W_SHIFT = 6
COLS = NP_ + W
LN_EPS = 1e-5
LOG_EPS = 1e-8
assert TAIL % CH == 0 and GROUPS % RING == 0 and TILES % 2 == 1 and 1 << W_SHIFT == W


def gnn_ffn(nc, x, src, dst, etype, w_rel, w_root, gnn_bias, ffn_w, ffn_b, out):
    fp32, bf16 = mybir.dt.float32, mybir.dt.bfloat16
    i32, u32, i16 = mybir.dt.int32, mybir.dt.uint32, mybir.dt.int16
    ALU = mybir.AluOpType
    ACT = mybir.ActivationFunctionType
    AX = mybir.AxisListType.X
    ds = bass.ds

    tables = [nc.dram_tensor(f"message_table{i}", [NP_ * R, D], fp32, kind="Internal").ap() for i in range(2)]
    span_dram = nc.dram_tensor("group_span", [2, GROUPS], fp32, kind="Internal").ap()
    batch_dram = nc.dram_tensor("tile_batches", [1, TILES], i32, kind="Internal").ap()
    tables_by_node = [table.rearrange("(n r) e -> n (r e)", r=R) for table in tables]

    ctx = ExitStack()
    with ctx:
        def sb(name, shape, dt):
            return ctx.enter_context(nc.sbuf_tensor(name, shape, dt))

        def pb(name, shape, dt=fp32):
            return ctx.enter_context(nc.psum_tensor(name, shape, dt))

        def sem(name):
            return ctx.enter_context(nc.semaphore(name))

        x_sb = sb("x_sb", [P, TILES, D], fp32)
        acc = sb("acc", [P, KH, COLS], fp32)
        wrel_sb = sb("wrel_sb", [P, KH, R * D], fp32)
        wroot_sb = sb("wroot_sb", [P, KH, D], fp32)
        bias_sb = sb("bias_sb", [P, KH], fp32)
        rows = sb("rows", [P, RING * CH * D], fp32)
        stage = sb("stage", [P, 2, R * D], fp32)
        idx_all = sb("idx_all", [P, (GROUPS + RING) * CH], i32)
        dst_all = sb("dst_all", [P, (GROUPS + 1) * CH], i16)
        node_iota = sb("node_iota", [P, COLS], i16)
        idx_ring = sb("idx_ring", [P, RING, CH], u32)
        onehot = sb("onehot", [P, 2, CH, W], fp32)
        xT = sb("xT", [P, 2, KH, P], fp32)
        xn = sb("xn", [P, 2, D], fp32)
        ident = sb("ident", [P, P], fp32)
        ident_bf = sb("ident_bf", [P, P], bf16)
        stats = sb("stats", [P, 2, 6], fp32)
        moments = sb("moments", [P, TILES + 1, 2], fp32)
        tile_moments = sb("tile_moments", [P, 2, 2], fp32)
        eps_col = sb("eps_col", [P, 1], fp32)
        base_row = sb("base_row", [1, GROUPS + 1], i32)
        extra_row = sb("extra_row", [1, GROUPS], i32)
        batch_row = sb("batch_row", [1, TILES + 1], i32)
        wT = sb("wT", [P, KH, D], fp32)
        wsT = sb("wsT", [P, KH, D], bf16)
        fbias_bc = sb("fbias_bc", [P, D], fp32)
        wmax = sb("wmax", [P, 4], fp32)
        spare = stage[:, 1, :]
        x1, mag, osgn = spare[:, 0:D], spare[:, D:2 * D], spare[:, 2 * D:3 * D]
        wmax_bc = spare[:, 5 * D:6 * D]
        magT = spare[:, 3 * D:4 * D].rearrange("p (h n) -> p h n", h=KH)
        sgn = spare[:, 4 * D:4 * D + P].bitcast(bf16)
        sgnT = spare[:, 4 * D + P:5 * D].bitcast(bf16).rearrange("p (h n) -> p h n", h=KH)
        mmax = sb("mmax", [P, 2], fp32)

        CW = GROUPS * CH
        raw = rows[:, :].bitcast(i32)
        src_raw, type_raw, dst_raw = raw[:, 0:CW], raw[:, CW:2 * CW], raw[:, 2 * CW:3 * CW]
        dst_rows = raw[:, 3 * CW:3 * CW + 2 * GE]
        at = 3 * CW + 2 * GE
        span = rows[:, at:at + 4]
        at += 4
        least, greatest = rows[0:1, at:at + GROUPS], rows[0:1, at + GROUPS:at + 2 * GROUPS]
        at += 2 * GROUPS
        least_by_tile = rows[0:TILES, at:at + GROUPS]
        tile_end = rows[0:TILES, at + GROUPS:at + GROUPS + 1]
        need = rows[0:TILES, at + GROUPS + 1:at + GROUPS + 2]
        batch_col = raw[0:TILES, at + GROUPS + 2:at + GROUPS + 3]
        group_no = node_iota[0:TILES, 1:GROUPS + 1]
        w_raw = onehot[:, :, :, :].rearrange("p a c w -> p (a c w)")[:, 0:KH * D].rearrange("p (h k) -> p h k", h=KH)
        w_sgn = spare[:, 3 * D:4 * D].bitcast(bf16).rearrange("p (h k) -> p h k", h=KH)
        ones = x1[:, 0:P]
        diag = mag[:, :].rearrange("p (h n) -> p h n", h=KH)

        banks = [pb(f"bank{i}", [P, 512]) for i in range(8)]
        seg = [banks[i][:, 0:KH * W].rearrange("p (h w) -> p h w", h=KH) for i in range(2)]
        rel = banks[2:6]
        root = banks[6][:, 0:KH * P].rearrange("p (h n) -> p h n", h=KH)
        tr = banks[7][:, 0:D]
        tr_h = tr.rearrange("p (h n) -> p h n", h=KH)
        mag_ps = rel[0][:, 0:D].rearrange("p (h n) -> p h n", h=KH)
        sgn_ps = rel[1][:, :].bitcast(bf16)[:, 0:D].rearrange("p (h n) -> p h n", h=KH)
        lns_ps = rel[2][:, 0:D]
        lns_sign_ps = rel[3][:, 0:D]

        x_loaded = [sem("x_head_loaded"), sem("x_loaded")]
        pads_set = sem("pads_set")
        edges_loaded = sem("edges_loaded")
        tail_loaded = sem("tail_loaded")
        setup = sem("setup")
        dst_rows_loaded = sem("dst_rows_loaded")
        span_ready = sem("span_ready")
        span_stored = sem("span_stored")
        span_loaded = sem("span_loaded")
        span_step = sem("span_step")
        batches_ready = sem("batches_ready")
        batches_stored = sem("batches_stored")
        batches_loaded = sem("batches_loaded")
        pool_ready = sem("pool_ready")
        ident_ready = sem("ident_ready")
        iota_ready = sem("iota_ready")
        weights_loaded = sem("weights_loaded")
        ffn_loaded = sem("ffn_loaded")
        w_ready = sem("w_ready")
        w_transposed = sem("w_transposed")
        w_taken = sem("w_taken")
        stats_ready = sem("stats_ready")
        moments_ready = sem("moments_ready")
        var_ready = sem("var_ready")
        std_ready = sem("std_ready")
        inv_ready = sem("inv_ready")
        xn_ready = sem("xn_ready")
        tr_ready = sem("tr_ready")
        xT_ready = sem("xT_ready")
        root_ready = sem("root_ready")
        root_used = sem("root_used")
        rel_ready = sem("rel_ready")
        rel_used = sem("rel_used")
        table_stored = sem("table_stored")
        gathered = [sem(f"gathered{i}") for i in range(RING)]
        onehot_ready = sem("onehot_ready")
        seg_ready = sem("seg_ready")
        acc_added = sem("acc_added")
        onehot_extra = sem("onehot_extra")
        seg_extra = sem("seg_extra")
        acc_extra = sem("acc_extra")
        group_done = sem("group_done")
        dve_mark, act_mark = sem("dve_mark"), sem("act_mark")
        pool_mark, pe_mark = sem("pool_mark"), sem("pe_mark")
        x1_ready = sem("x1_ready")
        dve_step = sem("dve_step")
        h_ready = sem("h_ready")
        h_transposed = sem("h_transposed")
        z_ready = sem("z_ready")
        mag_ready = sem("mag_ready")
        sgn_ready = sem("sgn_ready")
        mag_transposed = sem("mag_transposed")
        magT_ready = sem("magT_ready")
        sgnT_ready = sem("sgnT_ready")
        lns_ready = sem("lns_ready")
        osgn_ready = sem("osgn_ready")
        out_ready = sem("out_ready")
        out_stored = sem("out_stored")

        XA = 6
        x_full = x[0:(TILES - 1) * P, :].rearrange("(t p) d -> p t d", p=P)

        block = ctx.enter_context(nc.Block())

        @block.sync
        def _(sp):
            def load_weights(l):
                for h in range(KH):
                    sp.dma_start(
                        wrel_sb[:, h, :].rearrange("p (r e) -> p r e", r=R),
                        w_rel[ds(l, 1), :, h * P:(h + 1) * P, :].rearrange("o r p e -> (o p) r e"),
                    ).then_inc(weights_loaded, 16)
                sp.dma_start(wroot_sb[:, :, :],
                             w_root[ds(l, 1), :, :].rearrange("o (h p) e -> (o p) h e", p=P)).then_inc(weights_loaded, 16)
                with nc.allow_non_contiguous_dma(reason="256 bias values, one per partition and half"):
                    sp.dma_start(bias_sb[:, :],
                                 gnn_bias[ds(l, 1), :].rearrange("o (h p) -> (o p) h", p=P)).then_inc(weights_loaded, 16)

            sp.dma_start(x_sb[:, 0:XA, :], x_full[:, 0:XA, :]).then_inc(x_loaded[0], 16)
            load_weights(0)
            sp.wait_ge(pads_set, 1)
            sp.dma_start(x_sb[:, XA:TILES - 1, :], x_full[:, XA:TILES - 1, :]).then_inc(x_loaded[1], 16)
            sp.dma_start(x_sb[0:LAST_ROWS, TILES - 1, :], x[(TILES - 1) * P:N, :]).then_inc(x_loaded[1], 16)
            for to, of in ((src_raw, src), (type_raw, etype), (dst_raw, dst)):
                sp.dma_start(to[:, 0:FULL * CH].rearrange("p (g j) -> p g j", j=CH),
                             of[0:FULL * GE].rearrange("(g p j) -> p g j", p=P, j=CH)).then_inc(edges_loaded, 16)
            sp.dma_start(w_raw, ffn_w.rearrange("(h p) k -> p h k", p=P)).then_inc(ffn_loaded, 16)
            sp.dma_start(fbias_bc[:, :], ffn_b.unsqueeze(0).to_broadcast([P, D])).then_inc(ffn_loaded, 16)
            with sp.Fori(0, L - 1) as layer:
                sp.wait_ge(rel_used, 4 * (TILES * (layer + 1) + 1))
                sp.wait_ge(root_used, TILES * (layer + 1) + 1)
                load_weights(layer + 1)
            with sp.Fori(0, TILES - 1) as t:
                sp.wait_ge(out_ready, t + 1)
                sp.dma_start(out[ds(t * P, P), :],
                             x_sb[:, ds(t, 1), :].rearrange("p o d -> p (o d)")).then_inc(out_stored, 16)
            sp.wait_ge(out_ready, TILES)
            sp.dma_start(out[(TILES - 1) * P:N, :], x_sb[0:LAST_ROWS, TILES - 1, :]).then_inc(out_stored, 16)
            sp.wait_ge(out_stored, 16 * TILES)

        @block.gpsimd
        def _(pool):
            count = [0]

            def step(ins):
                count[0] += 1
                ins.then_inc(setup, 1)
                pool.wait_ge(setup, count[0])

            pad = slice(FULL * CH, CW)
            pool.memset(src_raw[:, pad], 0)
            pool.memset(type_raw[:, pad], 0)
            step(pool.memset(dst_raw[:, pad], -1))
            full = FULL * GE
            for to, of in ((src_raw, src), (type_raw, etype), (dst_raw, dst)):
                pool.dma_start(to[0:TAIL_P, pad],
                               of[full:E].rearrange("(p j) -> p j", j=CH)).then_inc(tail_loaded, 16)
            half = GROUPS // 2
            pool.dma_start(dst_rows[0:half - 1, :],
                           dst[0:(half - 1) * 2 * GE].rearrange("(p e) -> p e", p=half - 1)).then_inc(dst_rows_loaded, 16)
            pool.dma_start(dst_rows[half - 1:half, 0:GE], dst[(FULL - 1) * GE:full].unsqueeze(0)).then_inc(dst_rows_loaded, 16)
            pool.dma_start(dst_rows[half - 1:half, GE:2 * GE], dst[E - GE:E].unsqueeze(0)).then_inc(dst_rows_loaded, 16)
            step(pool.memset(ident[:, :], 1.0))
            step(pool.affine_select(ident[:, :], ident[:, :], pattern=[[1, P]], compare_op=ALU.is_equal,
                                    fill=0.0, base=0, channel_multiplier=-1))
            pool.tensor_copy(ident_bf[:, :], ident[:, :]).then_inc(ident_ready, 1)
            step(pool.iota(node_iota[:, :], pattern=[[1, COLS]], base=0, channel_multiplier=0))
            step(pool.iota(batch_col, pattern=[[0, 1]], base=P, channel_multiplier=P))
            pool.tensor_copy(tile_end, batch_col).then_inc(iota_ready, 1)
            pool.wait_ge(edges_loaded, 16 * 3)
            pool.wait_ge(tail_loaded, 16 * 3)
            step(pool.tensor_scalar(idx_all[:, 0:CW], src_raw, float(R), None, ALU.mult))
            step(pool.tensor_tensor(idx_all[:, 0:CW], idx_all[:, 0:CW], type_raw, ALU.add))
            step(pool.tensor_copy(idx_all[:, CW:], idx_all[:, 0:RING * CH]))
            step(pool.tensor_copy(dst_all[:, 0:CW], dst_raw))
            step(pool.tensor_copy(dst_all[:, CW:CW + CH], dst_raw[:, 0:CH]))
            step(pool.tensor_copy(idx_ring[:, :, :].rearrange("p i j -> p (i j)"), idx_all[:, 0:RING * CH]))
            half = GROUPS // 2
            pool.wait_ge(span_ready, 1)
            for m in range(2):
                pool.dma_start(span_dram[m, :].rearrange("(p a) -> p a", a=2),
                               span[0:half, 2 * m:2 * m + 2]).then_inc(span_stored, 16)
            pool.wait_ge(span_stored, 32)
            pool.dma_start(least, span_dram[0:1, :]).then_inc(span_loaded, 16)
            pool.dma_start(greatest, span_dram[1:2, :]).then_inc(span_loaded, 16)
            pool.dma_start(least_by_tile, span_dram[0:1, :].to_broadcast([TILES, GROUPS])).then_inc(span_loaded, 16)
            step(pool.memset(batch_row[:, 0:1], 0))
            pool.wait_ge(batches_ready, 1)
            pool.dma_start(batch_dram[0, :].unsqueeze(1), batch_col).then_inc(batches_stored, 16)
            pool.wait_ge(batches_stored, 16)
            pool.dma_start(batch_row[:, 1:TILES + 1], batch_dram[0:1, :]).then_inc(batches_loaded, 16)
            pool.wait_ge(batches_loaded, 16)
            pool.sem_inc(pool_ready, 1)
            pool.sem_inc(group_done, RING)

            for layer in range(L):
                pool.wait_ge(table_stored, 16 * (TILES * (layer + 1)))
                pool.sem_inc(pool_mark, 1)
                with pool.Fori(0, BATCHES) as b:
                    for i in range(RING):
                        pool.wait_ge(group_done, layer * GROUPS + b * RING + (i + 1))
                        pool.sem_inc(pool_mark, 1)
                        for j in range(CH):
                            s = (i * CH + j) * D
                            pool.indirect_dma_start(
                                rows[:, s:s + D], None, tables[layer % 2],
                                bass.IndirectOffsetOnAxis(ap=idx_ring[:, i, j:j + 1], axis=0),
                            ).then_inc(gathered[i], 16)

        @block.tensor
        def _(pe):
            def transposes(t, buf, first=False):
                pe.wait_ge(xn_ready, t + 1)
                if not first:
                    pe.wait_ge(xT_ready, t)
                for h in range(KH):
                    last = nc.tensor.transpose(tr_h[:, h, :], xn[:, buf, h * P:(h + 1) * P], ident[:, :])
                last.then_inc(tr_ready, 1)

            def transform(T, buf):
                pe.wait_ge(xT_ready, T + 1)
                pe.wait_ge(root_used, T + 1)
                for eh in range(KH):
                    for kh in range(KH):
                        last = nc.tensor.matmul(root[:, eh, :], wroot_sb[:, kh, eh * P:(eh + 1) * P],
                                                xT[:, buf, kh, :], start=(kh == 0), stop=(kh == KH - 1))
                last.then_inc(root_ready, 1)
                for b in range(4):
                    pe.wait_ge(rel_used, 4 * T + (b + 1))
                    for kh in range(KH):
                        last = nc.tensor.matmul(rel[b][:, :], xT[:, buf, kh, :], wrel_sb[:, kh, b * 512:(b + 1) * 512],
                                                start=(kh == 0), stop=(kh == KH - 1))
                    last.then_inc(rel_ready, 1)

            extras = pe.alloc_register("pe_extras")
            pe.reg_mov(extras, 0)

            def products(i):
                for h in range(KH):
                    for j in range(CH):
                        s = (i * CH + j) * D + h * P
                        last = nc.tensor.matmul(seg[i % 2][:, h, :], rows[:, s:s + P], onehot[:, i % 2, j, :],
                                                start=(j == 0), stop=(j == CH - 1))
                return last

            def batches(layer, t):
                first = pe.value_load(batch_row[0:1, ds(t, 1)], min_val=0, max_val=BATCHES)
                end = pe.value_load(batch_row[0:1, ds(t + 1, 1)], min_val=0, max_val=BATCHES)
                with pe.If(end > first):
                    with pe.Fori(first, end) as b:
                        for i in range(RING):
                            pe.wait_ge(onehot_ready, layer * GROUPS + b * RING + (i + 1))
                            pe.wait_ge(gathered[i], (layer * BATCHES + b + 1) * (16 * CH))
                            products(i).then_inc(seg_ready, 1)
                            more = pe.value_load(extra_row[0:1, ds(b * RING + i, 1)], min_val=0, max_val=N // W)
                            with pe.If(more > 0):
                                with pe.Fori(0, more):
                                    pe.wait_ge(onehot_extra, pe.snap(extras, min_val=0, max_val=1 << 20) + 1)
                                    products(i).then_inc(seg_extra, 1)
                                    pe.reg_add(extras, extras, 1)

            pe.wait_ge(ident_ready, 1)
            pe.wait_ge(weights_loaded, 64)
            transposes(0, 0, first=True)
            with pe.Fori(0, PAIRS) as i:
                transposes(2 * i + 1, 1)
                transform(2 * i, 0)
                transposes(2 * i + 2, 0)
                transform(2 * i + 1, 1)
            transform(TILES - 1, 0)

            pe.wait_ge(w_ready, 1)
            pe.wait_ge(rel_used, 4 * TILES + 4)
            pe.wait_ge(root_used, TILES + 1)
            for m in range(KH):
                for kh in range(KH):
                    nc.tensor.transpose(rel[m][:, kh * P:(kh + 1) * P], w_raw[:, m, kh * P:(kh + 1) * P], ident[:, :])
                    nc.tensor.transpose(rel[2 + m][:, :].bitcast(bf16)[:, kh * P:(kh + 1) * P],
                                        w_sgn[:, m, kh * P:(kh + 1) * P], ident_bf[:, :])
                last = nc.tensor.matmul(root[:, m, :], ones, diag[:, m, :], start=True, stop=True)
            last.then_inc(w_transposed, 1)
            pe.wait_ge(w_taken, 1)
            pe.wait_ge(pool_ready, 1)

            with pe.Fori(0, L - 1) as layer:
                pe.wait_ge(weights_loaded, 64 * (layer + 2))
                pe.sem_inc(pe_mark, 1)
                with pe.Fori(0, TILES) as t:
                    batches(layer, t)
                    transform(TILES * (layer + 1) + t, 0)

            with pe.Fori(0, TILES) as t:
                batches(L - 1, t)
                pe.wait_ge(h_ready, t + 1)
                for h in range(KH):
                    last = nc.tensor.transpose(tr_h[:, h, :], xT[:, 0, h, :], ident[:, :])
                last.then_inc(h_transposed, 1)
                pe.wait_ge(sgn_ready, t + 1)
                for h in range(KH):
                    nc.tensor.transpose(sgn_ps[:, h, :], sgn[:, h * P:(h + 1) * P], ident_bf[:, :])
                pe.wait_ge(mag_ready, t + 1)
                for h in range(KH):
                    last = nc.tensor.transpose(mag_ps[:, h, :], mag[:, h * P:(h + 1) * P], ident[:, :])
                last.then_inc(mag_transposed, 1)
                pe.wait_ge(sgnT_ready, t + 1)
                for h in range(KH):
                    nc.tensor.matmul(lns_sign_ps, sgnT[:, h, :], wsT[:, h, :], start=(h == 0), stop=(h == KH - 1))
                pe.wait_ge(magT_ready, t + 1)
                for h in range(KH):
                    last = nc.tensor.matmul(lns_ps, magT[:, h, :], wT[:, h, :], start=(h == 0), stop=(h == KH - 1))
                last.then_inc(lns_ready, 1)

        @block.scalar
        def _(act):
            def finish(T, t, buf, table=0, serial=False):
                act.wait_ge(root_ready, T + 1)
                act.sem_inc(act_mark, 1)
                for h in range(KH):
                    last = nc.scalar.activation(acc[:, h, ds(t * P, P)], root[:, h, :], ACT.Identity,
                                                bias=bias_sb[:, h:h + 1])
                last.then_inc(root_used, 1)
                if serial:
                    act.wait_ge(table_stored, 16 * T)
                for b in range(4):
                    act.wait_ge(rel_ready, 4 * T + (b + 1))
                    nc.scalar.copy(stage[:, buf, b * 512:(b + 1) * 512], rel[b][:, :]).then_inc(rel_used, 1)
                act.wait_ge(rel_used, 4 * (T + 2))
                act.dma_start(tables_by_node[table][ds(t * P, P), :], stage[:, buf, :]).then_inc(table_stored, 16)

            def deviations(lo, hi):
                return nc.scalar.activation(moments[:, lo:hi, 1:2], moments[:, lo:hi, 1:2], ACT.Sqrt, bias=eps_col[:, :])

            def take(t, buf):
                act.wait_ge(tr_ready, t + 1)
                nc.scalar.copy(xT[:, buf, :, :], tr_h).then_inc(xT_ready, 1)

            act.sem_inc(root_used, 1)
            act.sem_inc(rel_used, 4)
            act.wait_ge(weights_loaded, 64)
            act.wait_ge(pads_set, 2)
            act.wait_ge(var_ready, 1)
            deviations(0, XA).then_inc(std_ready, 1)
            take(0, 0)

            def pair(t, others=None):
                take(t + 1, 1)
                finish(t, t, 0)
                if others:
                    others()
                act.wait_ge(table_stored, 16 * (t + 1))
                take(t + 2, 0)
                finish(t + 1, t + 1, 1)
                act.wait_ge(table_stored, 16 * (t + 2))

            def rest():
                act.wait_ge(var_ready, 2)
                deviations(XA, TILES).then_inc(std_ready, 1)

            for i in range(XA // 2):
                pair(2 * i, rest if i == XA // 2 - 1 else None)
            with act.Fori(XA // 2, PAIRS) as i:
                pair(2 * i)
            finish(TILES - 1, TILES - 1, 0)

            act.wait_ge(w_transposed, 1)
            act.wait_ge(pool_ready, 1)
            act.wait_ge(ffn_loaded, 32)
            for m in range(KH):
                nc.scalar.copy(wT[:, :, m * P:(m + 1) * P], rel[m][:, 0:D].rearrange("p (h n) -> p h n", h=KH))
                nc.scalar.copy(wsT[:, :, m * P:(m + 1) * P],
                               rel[2 + m][:, :].bitcast(bf16)[:, 0:D].rearrange("p (h n) -> p h n", h=KH))
            nc.scalar.copy(wmax_bc.rearrange("p (h n) -> p h n", h=KH), root).then_inc(w_taken, 1)

            def rectified(layer, t):
                end = act.value_load(batch_row[0:1, ds(t + 1, 1)], min_val=0, max_val=BATCHES)
                act.wait_ge(group_done, layer * GROUPS + end * RING + RING)
                act.sem_inc(act_mark, 1)
                return nc.scalar.activation(xT[:, 0, :, :], acc[:, :, ds(t * P, P)], ACT.Relu)

            for layer in range(L - 1):
                act.wait_ge(weights_loaded, 64 * (layer + 2))
                with act.Fori(0, TILES) as t:
                    rectified(layer, t).then_inc(xT_ready, 1)
                    finish(TILES * (layer + 1) + t, t, 0, (layer + 1) % 2, serial=True)
            with act.Fori(0, TILES) as t:
                rectified(L - 1, t).then_inc(h_ready, 1)
                act.wait_ge(var_ready, t + 3)
                deviations(TILES, TILES + 1).then_inc(std_ready, 1)
                act.wait_ge(z_ready, t + 1)
                nc.scalar.activation(sgn, xn[:, 0, :], ACT.Sign).then_inc(sgn_ready, 1)
                act.wait_ge(mag_transposed, t + 1)
                nc.scalar.copy(magT, mag_ps).then_inc(magT_ready, 1)
                act.wait_ge(lns_ready, t + 1)
                nc.scalar.activation(osgn, lns_sign_ps, ACT.Sign).then_inc(osgn_ready, 1)

        @block.vector
        def _(dve):
            def chained(base, k, ins):
                ins.then_inc(dve_step, 1)
                dve.wait_ge(dve_step, base + k)

            def tile_of(t):
                return x_sb[:, ds(t, 1), :].rearrange("p o d -> p (o d)")

            def tile_stats(t, buf):
                nc.vector.bn_stats(stats[:, buf, :], tile_of(t)).then_inc(stats_ready, 1)
                dve.wait_ge(stats_ready, t + 1)
                dve.sem_inc(dve_mark, 1)
                nc.vector.bn_aggr(tile_moments[:, buf, :], stats[:, buf, :]).then_inc(moments_ready, 1)
                dve.wait_ge(moments_ready, t + 1)
                return nc.vector.tensor_copy(moments[:, ds(t, 1), :].rearrange("p o a -> p (o a)"), tile_moments[:, buf, :])

            def inverse(lo, hi):
                return nc.vector.reciprocal(moments[:, lo:hi, 1:2], moments[:, lo:hi, 1:2])

            def norm_tile(t, buf, wait=True):
                if wait:
                    dve.wait_ge(tr_ready, t - 1)
                scalars = moments[:, ds(t, 1), :].rearrange("p o a -> p (o a)")
                nc.vector.tensor_scalar(xn[:, buf, :], tile_of(t), scalars[:, 0:1], scalars[:, 1:2],
                                        ALU.subtract, ALU.mult).then_inc(xn_ready, 1)

            nc.vector.memset(x_sb[:, TILES - 1, :], 0.0).then_inc(pads_set, 1)
            nc.vector.memset(eps_col[:, :], LN_EPS).then_inc(pads_set, 1)
            nc.vector.memset(acc[:, :, NP_:], 0.0)
            dve.wait_ge(x_loaded[0], 16)
            for t in range(XA - 1):
                tile_stats(t, t % 2)
            tile_stats(XA - 1, 1).then_inc(var_ready, 1)
            dve.wait_ge(std_ready, 1)
            inverse(0, XA).then_inc(inv_ready, 1)
            dve.wait_ge(inv_ready, 1)
            norm_tile(0, 0, wait=False)
            norm_tile(1, 1, wait=False)
            for t in range(2, XA):
                norm_tile(t, t % 2)
            dve.wait_ge(x_loaded[1], 32)
            with dve.Fori(XA, TILES - 1) as t:
                tile_stats(t, 0)
            tile_stats(TILES - 1, 0).then_inc(var_ready, 1)
            dve.wait_ge(std_ready, 2)
            inverse(XA, TILES).then_inc(inv_ready, 1)
            dve.wait_ge(inv_ready, 2)
            dve.wait_ge(dst_rows_loaded, 16 * 3)
            by_group = dst_rows[0:GROUPS // 2, :].rearrange("p (a e) -> p a e", a=2)
            nc.vector.tensor_reduce(span[0:GROUPS // 2, 0:2], by_group, axis=AX, op=ALU.min)
            nc.vector.tensor_reduce(span[0:GROUPS // 2, 2:4], by_group, axis=AX, op=ALU.max).then_inc(span_ready, 1)
            MID = PAIRS // 2
            with dve.Fori(XA // 2, MID) as i:
                norm_tile(2 * i, 0)
                norm_tile(2 * i + 1, 1)

            def span_link(k, ins):
                ins.then_inc(span_step, 1)
                dve.wait_ge(span_step, k)

            dve.wait_ge(span_loaded, 16 * 3)
            dve.wait_ge(iota_ready, 1)
            nc.vector.tensor_copy(base_row[:, 0:GROUPS], least)
            nc.vector.tensor_copy(base_row[:, GROUPS:GROUPS + 1], least[:, 0:1])
            span_link(1, nc.vector.tensor_tensor(extra_row[:, :], greatest, least, ALU.subtract))
            span_link(2, nc.vector.tensor_single_scalar(extra_row[:, :], extra_row[:, :], W_SHIFT, ALU.arith_shift_right))
            span_link(3, nc.vector.scalar_tensor_tensor(least_by_tile, least_by_tile, tile_end, group_no, ALU.is_lt, ALU.mult))
            span_link(4, nc.vector.reduce_max(need, least_by_tile, AX))
            span_link(5, nc.vector.tensor_scalar(batch_col, need, float(RING - 1), None, ALU.add))
            nc.vector.tensor_single_scalar(batch_col, batch_col, RING.bit_length() - 1, ALU.arith_shift_right).then_inc(batches_ready, 1)
            with dve.Fori(MID, PAIRS) as i:
                norm_tile(2 * i, 0)
                norm_tile(2 * i + 1, 1)
            norm_tile(TILES - 1, 0)

            base = 0
            dve.wait_ge(ffn_loaded, 32)
            dve.wait_ge(table_stored, 16 * (TILES - 1))
            chained(base, 1, nc.vector.memset(ones, 1.0))
            k = 1
            for h in range(KH):
                chained(base, k + 1, nc.vector.tensor_single_scalar(w_sgn[:, h, :], w_raw[:, h, :], 0.0, ALU.is_lt))
                chained(base, k + 2, nc.vector.scalar_tensor_tensor(w_sgn[:, h, :], w_raw[:, h, :], 0.0, w_sgn[:, h, :], ALU.is_gt, ALU.subtract))
                chained(base, k + 3, nc.vector.scalar_tensor_tensor(mag, w_raw[:, h, :], -1.0, w_raw[:, h, :], ALU.mult, ALU.max))
                chained(base, k + 4, nc.vector.tensor_scalar(w_raw[:, h, :], mag, LOG_EPS, None, ALU.add))
                chained(base, k + 5, nc.vector.reduce_max(wmax[:, h:h + 1], w_raw[:, h, :], AX))
                chained(base, k + 6, nc.vector.reciprocal(wmax[:, 2 + h:3 + h], wmax[:, h:h + 1]))
                chained(base, k + 7, nc.vector.tensor_scalar(w_raw[:, h, :], w_raw[:, h, :], wmax[:, 2 + h:3 + h], None, ALU.mult))
                k += 7
            dve.wait_ge(ident_ready, 1)
            for h in range(KH):
                last = nc.vector.tensor_scalar(diag[:, h, :], ident[:, :], wmax[:, h:h + 1], None, ALU.mult)
            last.then_inc(w_ready, 1)
            base += k
            dve.wait_ge(w_taken, 1)
            dve.wait_ge(pool_ready, 1)

            extras = dve.alloc_register("dve_extras")
            dve.reg_mov(extras, 0)

            def make_onehot(buf, first_node, g):
                return nc.vector.tensor_tensor(
                    onehot[:, buf, :, :],
                    node_iota[:, ds(first_node, W)].unsqueeze(1).to_broadcast([P, CH, W]),
                    dst_all[:, ds(g * CH, CH)].unsqueeze(2).to_broadcast([P, CH, W]), ALU.is_equal)

            def add(buf, first_node):
                cols = acc[:, :, ds(first_node, W)]
                return nc.vector.tensor_tensor(cols, cols, seg[buf], ALU.add)

            def base_of(g):
                return dve.value_load(base_row[0:1, ds(g, 1)], min_val=0, max_val=N - 1)

            def batch(layer, b):
                for i in range(RING):
                    g = b * RING + i
                    q = layer * GROUPS + g
                    make_onehot((i + 1) % 2, base_of(g + 1), g + 1).then_inc(onehot_ready, 1)
                    first = base_of(g)
                    dve.wait_ge(seg_ready, q + 1)
                    add(i % 2, first).then_inc(acc_added, 1)
                    dve.wait_ge(acc_added, q + 1)
                    more = dve.value_load(extra_row[0:1, ds(g, 1)], min_val=0, max_val=N // W)
                    with dve.If(more > 0):
                        with dve.Fori(1, more + 1) as k:
                            node = nc.s_assert_within(first + k * W, 0, N - 1, skip_runtime_bounds_check_because="k * W is at most the span of the group")
                            done = dve.snap(extras, min_val=0, max_val=1 << 20)
                            make_onehot(i % 2, node, g).then_inc(onehot_extra, 1)
                            dve.wait_ge(seg_extra, done + 1)
                            add(i % 2, node).then_inc(acc_extra, 1)
                            dve.wait_ge(acc_extra, done + 1)
                            dve.reg_add(extras, extras, 1)
                    nc.vector.tensor_copy(idx_ring[:, i, :], idx_all[:, ds((g + RING) * CH, CH)]).then_inc(group_done, 1)

            make_onehot(0, base_of(0), 0).then_inc(onehot_ready, 1)
            with dve.Fori(0, L - 1) as layer:
                with dve.Fori(0, BATCHES) as b:
                    batch(layer, b)
            with dve.Fori(0, TILES) as t:
                start = dve.value_load(batch_row[0:1, ds(t, 1)], min_val=0, max_val=BATCHES)
                end = dve.value_load(batch_row[0:1, ds(t + 1, 1)], min_val=0, max_val=BATCHES)
                with dve.If(end > start):
                    with dve.Fori(start, end) as b:
                        batch(L - 1, b)
                c = base + t * 7
                dve.wait_ge(h_transposed, t + 1)
                nc.vector.tensor_tensor(x1, tile_of(t), tr, ALU.add).then_inc(x1_ready, 1)
                dve.wait_ge(x1_ready, t + 1)
                nc.vector.bn_stats(stats[:, 0, :], x1).then_inc(stats_ready, 1)
                dve.wait_ge(stats_ready, TILES + t + 1)
                dve.sem_inc(dve_mark, 1)
                nc.vector.bn_aggr(moments[:, TILES, :], stats[:, 0, :]).then_inc(var_ready, 1)
                dve.wait_ge(std_ready, t + 3)
                inverse(TILES, TILES + 1).then_inc(inv_ready, 1)
                dve.wait_ge(inv_ready, t + 3)
                nc.vector.tensor_scalar(xn[:, 0, :], x1, moments[:, TILES, 0:1], moments[:, TILES, 1:2],
                                        ALU.subtract, ALU.mult).then_inc(z_ready, 1)
                dve.wait_ge(z_ready, t + 1)
                chained(c, 1, nc.vector.scalar_tensor_tensor(mag, xn[:, 0, :], -1.0, xn[:, 0, :], ALU.mult, ALU.max))
                chained(c, 2, nc.vector.tensor_scalar(mag, mag, LOG_EPS, None, ALU.add))
                chained(c, 3, nc.vector.reduce_max(mmax[:, 0:1], mag, AX))
                chained(c, 4, nc.vector.reciprocal(mmax[:, 1:2], mmax[:, 0:1]))
                nc.vector.tensor_scalar(mag, mag, mmax[:, 1:2], None, ALU.mult).then_inc(mag_ready, 1)
                chained(c, 5, nc.vector.tensor_tensor(x1, x1, fbias_bc[:, :], ALU.add))
                dve.wait_ge(mag_transposed, t + 1)
                nc.vector.tensor_copy(sgnT, sgn_ps).then_inc(sgnT_ready, 1)
                dve.wait_ge(lns_ready, t + 1)
                chained(c, 6, nc.vector.scalar_tensor_tensor(mag, lns_ps, mmax[:, 0:1], wmax_bc, ALU.mult, ALU.mult))
                dve.wait_ge(osgn_ready, t + 1)
                chained(c, 7, nc.vector.tensor_tensor(mag, mag, osgn, ALU.mult))
                nc.vector.tensor_tensor(tile_of(t), mag, x1, ALU.add).then_inc(out_ready, 1)
                dve.wait_ge(out_ready, t + 1)


_INS = ["x", "src", "dst", "edge_type_8", "L0_gnn_W_rel", "L0_gnn_W_root", "L0_gnn_bias", "L0_ffn_weight", "L0_ffn_bias"]
_OUTS = [((N, D), "float32")]


def kernel(**inputs):
    import numpy as _np
    import concourse.bacc as _bacc
    from concourse import mybir as _mybir
    from concourse.bass_utils import run_bass_kernel_spmd as _run

    nc = _bacc.Bacc("TRN2", target_bir_lowering=False, num_devices=1)
    arrays, args = {}, []
    for name in _INS:
        a = _np.ascontiguousarray(inputs[name])
        arrays[f"in_{name}_dram"] = a
        args.append(nc.dram_tensor(f"in_{name}_dram", a.shape, _mybir.dt.from_np(a.dtype), kind="ExternalInput").ap())
    for i, (shape, dtype) in enumerate(_OUTS):
        dt = _mybir.dt.from_np(_np.dtype(dtype))
        args.append(nc.dram_tensor(f"out_{i}_dram", shape, dt, kind="ExternalOutput").ap())
    gnn_ffn(nc, *args)
    r = _run(nc, [arrays], core_ids=[0])
    got = tuple(r.results[0][f"out_{i}_dram"] for i in range(len(_OUTS)))
    return got[0]
```

```python
from contextlib import ExitStack

import concourse.bass as bass
from concourse import mybir

N, D, E, R, L = 6250, 256, 200000, 8, 3
P = 128
KH = D // P
TILES = -(-N // P)
PAIRS = TILES // 2
LAST_ROWS = N - (TILES - 1) * P
NP_ = TILES * P
CH = 8
GE = CH * P
GROUPS = -(-E // GE)
FULL = E // GE
TAIL = E - FULL * GE
TAIL_P = TAIL // CH
RING = 4
BATCHES = GROUPS // RING
W = 64
W_SHIFT = 6
COLS = NP_ + W
XC = 12
XCHUNKS = 4
LN_EPS = 1e-5
LOG_EPS = 1e-8
assert TILES == XC * XCHUNKS + 1 and XC % 2 == 0 and TAIL % CH == 0 and GROUPS % RING == 0 and TILES % 2 == 1 and 1 << W_SHIFT == W


def gnn_ffn(nc, x, src, dst, etype, w_rel, w_root, gnn_bias, ffn_w, ffn_b, out):
    fp32, bf16 = mybir.dt.float32, mybir.dt.bfloat16
    f32r = mybir.dt.float32r
    i32, u32, i16 = mybir.dt.int32, mybir.dt.uint32, mybir.dt.int16
    ALU = mybir.AluOpType
    ACT = mybir.ActivationFunctionType
    AX = mybir.AxisListType.X
    ds = bass.ds

    tables = [nc.dram_tensor(f"message_table{i}", [NP_ * R, D], fp32, kind="Internal").ap() for i in range(2)]
    span_dram = nc.dram_tensor("group_span", [2, GROUPS], fp32, kind="Internal").ap()
    batch_dram = nc.dram_tensor("tile_batches", [1, TILES], i32, kind="Internal").ap()
    tables_by_node = [table.rearrange("(n r) e -> n (r e)", r=R) for table in tables]

    ctx = ExitStack()
    with ctx:
        def sb(name, shape, dt):
            return ctx.enter_context(nc.sbuf_tensor(name, shape, dt))

        def pb(name, shape, dt=fp32):
            return ctx.enter_context(nc.psum_tensor(name, shape, dt))

        def sem(name):
            return ctx.enter_context(nc.semaphore(name))

        x_sb = sb("x_sb", [P, TILES, D], fp32)
        arena = nc.sbuf_base
        acc = sb("acc", [P, KH, COLS], fp32)
        def in_arena(name, shape, at_bytes):
            return nc.alloc_sbuf_tensor_at(name, shape, f32r, offset=arena + at_bytes)

        w_hi = in_arena("w_hi", [P, KH, R * D], 0)
        w_lo = in_arena("w_lo", [P, KH, R * D], 4 * KH * R * D)
        x_hi = in_arena("x_hi", [P, 2, KH, P], 8 * KH * R * D)
        x_lo = in_arena("x_lo", [P, 2, KH, P], 8 * KH * R * D + 8 * KH * P)
        wrel_sb = sb("wrel_sb", [P, KH, R * D], fp32)
        wroot_sb = sb("wroot_sb", [P, KH, D], fp32)
        bias_sb = sb("bias_sb", [P, KH], fp32)
        rows = sb("rows", [P, RING * CH * D], fp32)
        stage = sb("stage", [P, 2, R * D], fp32)
        idx_all = sb("idx_all", [P, (GROUPS + RING) * CH], i32)
        dst_all = sb("dst_all", [P, (GROUPS + 1) * CH], i16)
        node_iota = sb("node_iota", [P, COLS], i16)
        idx_ring = sb("idx_ring", [P, RING, CH], u32)
        onehot = sb("onehot", [P, 2, CH, W], fp32)
        xT = sb("xT", [P, KH, P], fp32)
        xn = sb("xn", [P, 2, D], fp32)
        ident = sb("ident", [P, P], fp32)
        ident_bf = sb("ident_bf", [P, P], bf16)
        stats = sb("stats", [P, 2, 6], fp32)
        moments = sb("moments", [P, TILES + 1, 2], fp32)
        tile_moments = sb("tile_moments", [P, 2, 2], fp32)
        eps_col = sb("eps_col", [P, 1], fp32)
        base_row = sb("base_row", [1, GROUPS + 1], i32)
        extra_row = sb("extra_row", [1, GROUPS], i32)
        batch_row = sb("batch_row", [1, TILES + 1], i32)
        wT = sb("wT", [P, KH, D], fp32)
        wsT = sb("wsT", [P, KH, D], bf16)
        wmax_bc = sb("wmax_bc", [P, D], fp32)
        fbias_bc = sb("fbias_bc", [P, D], fp32)
        wmax = sb("wmax", [P, 4], fp32)
        spare = stage[:, 1, :]
        x1, mag, osgn = spare[:, 0:D], spare[:, D:2 * D], spare[:, 2 * D:3 * D]
        magT = spare[:, 3 * D:4 * D].rearrange("p (h n) -> p h n", h=KH)
        sgn = spare[:, 4 * D:4 * D + P].bitcast(bf16)
        sgnT = spare[:, 4 * D + P:5 * D].bitcast(bf16).rearrange("p (h n) -> p h n", h=KH)
        mmax = sb("mmax", [P, 2], fp32)

        CW = GROUPS * CH
        raw = rows[:, :].bitcast(i32)
        src_raw, type_raw, dst_raw = raw[:, 0:CW], raw[:, CW:2 * CW], raw[:, 2 * CW:3 * CW]
        dst_rows = raw[:, 3 * CW:3 * CW + 2 * GE]
        at = 3 * CW + 2 * GE
        span = rows[:, at:at + 4]
        at += 4
        least, greatest = rows[0:1, at:at + GROUPS], rows[0:1, at + GROUPS:at + 2 * GROUPS]
        at += 2 * GROUPS
        least_by_tile = rows[0:TILES, at:at + GROUPS]
        tile_end = rows[0:TILES, at + GROUPS:at + GROUPS + 1]
        need = rows[0:TILES, at + GROUPS + 1:at + GROUPS + 2]
        batch_col = raw[0:TILES, at + GROUPS + 2:at + GROUPS + 3]
        group_no = node_iota[0:TILES, 1:GROUPS + 1]
        w_raw = onehot[:, :, :, :].rearrange("p a c w -> p (a c w)")[:, 0:KH * D].rearrange("p (h k) -> p h k", h=KH)
        w_sgn = spare[:, 3 * D:4 * D].bitcast(bf16).rearrange("p (h k) -> p h k", h=KH)
        ones = x1[:, 0:P]
        diag = mag[:, :].rearrange("p (h n) -> p h n", h=KH)

        banks = [pb(f"bank{i}", [P, 512]) for i in range(8)]
        seg = [banks[i][:, 0:KH * W].rearrange("p (h w) -> p h w", h=KH) for i in range(2)]
        rel = banks[2:6]
        roots = [banks[6 + i][:, 0:KH * P].rearrange("p (h n) -> p h n", h=KH) for i in range(2)]
        tr = banks[7][:, 0:D]
        tr_h = tr.rearrange("p (h n) -> p h n", h=KH)
        mag_ps = rel[0][:, 0:D].rearrange("p (h n) -> p h n", h=KH)
        sgn_ps = rel[1][:, :].bitcast(bf16)[:, 0:D].rearrange("p (h n) -> p h n", h=KH)
        lns_ps = rel[2][:, 0:D]
        lns_sign_ps = rel[3][:, 0:D]

        x_loaded = [sem(f"x_loaded{c}") for c in range(XCHUNKS)]
        x_reloaded = sem("x_reloaded")
        pads_set = sem("pads_set")
        edges_loaded = sem("edges_loaded")
        tail_loaded = sem("tail_loaded")
        setup = sem("setup")
        dst_rows_loaded = sem("dst_rows_loaded")
        span_ready = sem("span_ready")
        span_stored = sem("span_stored")
        span_loaded = sem("span_loaded")
        span_step = sem("span_step")
        batches_ready = sem("batches_ready")
        batches_stored = sem("batches_stored")
        batches_loaded = sem("batches_loaded")
        pool_ready = sem("pool_ready")
        ident_ready = sem("ident_ready")
        iota_ready = sem("iota_ready")
        rel_loaded = sem("rel_loaded")
        root_loaded = sem("root_loaded")
        w_hi_ready = sem("w_hi_ready")
        w_lo_ready = sem("w_lo_ready")
        ffn_loaded = sem("ffn_loaded")
        fbias_loaded = sem("fbias_loaded")
        w_ready = sem("w_ready")
        w_transposed = sem("w_transposed")
        w_taken = sem("w_taken")
        stats_ready = sem("stats_ready")
        moments_ready = sem("moments_ready")
        var_ready = sem("var_ready")
        std_ready = sem("std_ready")
        inv_ready = sem("inv_ready")
        xn_ready = sem("xn_ready")
        tr_ready = sem("tr_ready")
        xT_ready = sem("xT_ready")
        root_ready = sem("root_ready")
        root_used = sem("root_used")
        rel_ready = sem("rel_ready")
        rel_used = sem("rel_used")
        stored = [sem("stored0"), sem("stored1")]
        hi_ready = sem("hi_ready")
        lo_ready = sem("lo_ready")
        gathered = [sem(f"gathered{i}") for i in range(RING)]
        onehot_ready = sem("onehot_ready")
        seg_ready = sem("seg_ready")
        acc_added = sem("acc_added")
        onehot_extra = sem("onehot_extra")
        seg_extra = sem("seg_extra")
        acc_extra = sem("acc_extra")
        group_done = sem("group_done")
        dve_mark, act_mark = sem("dve_mark"), sem("act_mark")
        pool_mark, pe_mark = sem("pool_mark"), sem("pe_mark")
        x1_ready = sem("x1_ready")
        dve_step = sem("dve_step")
        h_ready = sem("h_ready")
        h_transposed = sem("h_transposed")
        z_ready = sem("z_ready")
        mag_ready = sem("mag_ready")
        sgn_ready = sem("sgn_ready")
        mag_transposed = sem("mag_transposed")
        magT_ready = sem("magT_ready")
        sgnT_ready = sem("sgnT_ready")
        lns_ready = sem("lns_ready")
        osgn_ready = sem("osgn_ready")
        out_ready = sem("out_ready")
        out_stored = sem("out_stored")

        chunks = [(c * XC, (c + 1) * XC) for c in range(XCHUNKS - 1)] + [((XCHUNKS - 1) * XC, TILES)]
        x_full = x[0:(TILES - 1) * P, :].rearrange("(t p) d -> p t d", p=P)

        block = ctx.enter_context(nc.Block())

        @block.sync
        def _(sp):
            def load_rel(l):
                for h in range(KH):
                    sp.dma_start(
                        wrel_sb[:, h, :].rearrange("p (r e) -> p r e", r=R),
                        w_rel[ds(l, 1), :, h * P:(h + 1) * P, :].rearrange("o r p e -> (o p) r e"),
                    ).then_inc(rel_loaded, 16)

            def load_root(l):
                sp.dma_start(wroot_sb[:, :, :],
                             w_root[ds(l, 1), :, :].rearrange("o (h p) e -> (o p) h e", p=P)).then_inc(root_loaded, 16)
                with nc.allow_non_contiguous_dma(reason="256 bias values, one per partition and half"):
                    sp.dma_start(bias_sb[:, :],
                                 gnn_bias[ds(l, 1), :].rearrange("o (h p) -> (o p) h", p=P)).then_inc(root_loaded, 16)

            sp.dma_start(w_raw, ffn_w.rearrange("(h p) k -> p h k", p=P)).then_inc(ffn_loaded, 16)
            load_rel(0)
            for c, (lo, hi) in enumerate(chunks):
                end = min(hi, TILES - 1)
                sp.dma_start(x_sb[:, lo:end, :], x_full[:, lo:end, :]).then_inc(x_loaded[c], 16)
            sp.wait_ge(pads_set, 1)
            sp.dma_start(x_sb[0:LAST_ROWS, TILES - 1, :], x[(TILES - 1) * P:N, :]).then_inc(x_loaded[-1], 16)
            sp.dma_start(fbias_bc[:, :], ffn_b.unsqueeze(0).to_broadcast([P, D])).then_inc(fbias_loaded, 16)
            for to, of in ((src_raw, src), (type_raw, etype), (dst_raw, dst)):
                sp.dma_start(to[:, 0:FULL * CH].rearrange("p (g j) -> p g j", j=CH),
                             of[0:FULL * GE].rearrange("(g p j) -> p g j", p=P, j=CH)).then_inc(edges_loaded, 16)
            load_root(0)
            sp.wait_ge(w_lo_ready, KH)
            load_rel(1)
            sp.wait_ge(root_used, TILES + 2)
            load_root(1)
            sp.dma_start(x_sb[:, 0:TILES - 1, :], x_full).then_inc(x_reloaded, 16)
            sp.dma_start(x_sb[0:LAST_ROWS, TILES - 1, :], x[(TILES - 1) * P:N, :]).then_inc(x_reloaded, 16)
            sp.wait_ge(rel_used, 4 * (2 * TILES + 1))
            load_rel(2)
            sp.wait_ge(root_used, 2 * TILES + 2)
            load_root(2)
            with sp.Fori(0, TILES - 1) as t:
                sp.wait_ge(out_ready, t + 1)
                sp.dma_start(out[ds(t * P, P), :],
                             x_sb[:, ds(t, 1), :].rearrange("p o d -> p (o d)")).then_inc(out_stored, 16)
            sp.wait_ge(out_ready, TILES)
            sp.dma_start(out[(TILES - 1) * P:N, :], x_sb[0:LAST_ROWS, TILES - 1, :]).then_inc(out_stored, 16)
            sp.wait_ge(out_stored, 16 * TILES)

        @block.gpsimd
        def _(pool):
            count = [0]

            def step(ins):
                count[0] += 1
                ins.then_inc(setup, 1)
                pool.wait_ge(setup, count[0])

            step(pool.memset(ident[:, :], 1.0))
            step(pool.affine_select(ident[:, :], ident[:, :], pattern=[[1, P]], compare_op=ALU.is_equal,
                                    fill=0.0, base=0, channel_multiplier=-1))
            pool.tensor_copy(ident_bf[:, :], ident[:, :]).then_inc(ident_ready, 1)
            pad = slice(FULL * CH, CW)
            pool.memset(src_raw[:, pad], 0)
            pool.memset(type_raw[:, pad], 0)
            step(pool.memset(dst_raw[:, pad], -1))
            full = FULL * GE
            for to, of in ((src_raw, src), (type_raw, etype), (dst_raw, dst)):
                pool.dma_start(to[0:TAIL_P, pad],
                               of[full:E].rearrange("(p j) -> p j", j=CH)).then_inc(tail_loaded, 16)
            half = GROUPS // 2
            pool.dma_start(dst_rows[0:half - 1, :],
                           dst[0:(half - 1) * 2 * GE].rearrange("(p e) -> p e", p=half - 1)).then_inc(dst_rows_loaded, 16)
            pool.dma_start(dst_rows[half - 1:half, 0:GE], dst[(FULL - 1) * GE:full].unsqueeze(0)).then_inc(dst_rows_loaded, 16)
            pool.dma_start(dst_rows[half - 1:half, GE:2 * GE], dst[E - GE:E].unsqueeze(0)).then_inc(dst_rows_loaded, 16)
            step(pool.iota(node_iota[:, :], pattern=[[1, COLS]], base=0, channel_multiplier=0))
            step(pool.iota(batch_col, pattern=[[0, 1]], base=P, channel_multiplier=P))
            pool.tensor_copy(tile_end, batch_col).then_inc(iota_ready, 1)
            pool.wait_ge(edges_loaded, 16 * 3)
            pool.wait_ge(tail_loaded, 16 * 3)
            step(pool.tensor_scalar(idx_all[:, 0:CW], src_raw, float(R), None, ALU.mult))
            step(pool.tensor_tensor(idx_all[:, 0:CW], idx_all[:, 0:CW], type_raw, ALU.add))
            step(pool.tensor_copy(idx_all[:, CW:], idx_all[:, 0:RING * CH]))
            step(pool.tensor_copy(dst_all[:, 0:CW], dst_raw))
            step(pool.tensor_copy(dst_all[:, CW:CW + CH], dst_raw[:, 0:CH]))
            step(pool.tensor_copy(idx_ring[:, :, :].rearrange("p i j -> p (i j)"), idx_all[:, 0:RING * CH]))
            half = GROUPS // 2
            pool.wait_ge(span_ready, 1)
            for m in range(2):
                pool.dma_start(span_dram[m, :].rearrange("(p a) -> p a", a=2),
                               span[0:half, 2 * m:2 * m + 2]).then_inc(span_stored, 16)
            pool.wait_ge(span_stored, 32)
            pool.dma_start(least, span_dram[0:1, :]).then_inc(span_loaded, 16)
            pool.dma_start(greatest, span_dram[1:2, :]).then_inc(span_loaded, 16)
            pool.dma_start(least_by_tile, span_dram[0:1, :].to_broadcast([TILES, GROUPS])).then_inc(span_loaded, 16)
            step(pool.memset(batch_row[:, 0:1], 0))
            pool.wait_ge(batches_ready, 1)
            pool.dma_start(batch_dram[0, :].unsqueeze(1), batch_col).then_inc(batches_stored, 16)
            pool.wait_ge(batches_stored, 16)
            pool.dma_start(batch_row[:, 1:TILES + 1], batch_dram[0:1, :]).then_inc(batches_loaded, 16)
            pool.wait_ge(batches_loaded, 16)
            pool.sem_inc(pool_ready, 1)
            pool.sem_inc(group_done, RING)

            for layer in range(L):
                pool.wait_ge(stored[0], 16 * (PAIRS + 1 + TILES * layer))
                if layer == 0:
                    pool.wait_ge(stored[1], 16 * PAIRS)
                pool.sem_inc(pool_mark, 1)
                with pool.Fori(0, BATCHES) as b:
                    for i in range(RING):
                        pool.wait_ge(group_done, layer * GROUPS + b * RING + (i + 1))
                        pool.sem_inc(pool_mark, 1)
                        for j in range(CH):
                            s = (i * CH + j) * D
                            pool.indirect_dma_start(
                                rows[:, s:s + D], None, tables[layer % 2],
                                bass.IndirectOffsetOnAxis(ap=idx_ring[:, i, j:j + 1], axis=0),
                            ).then_inc(gathered[i], 16)

        @block.tensor
        def _(pe):
            def transposes(t, buf, first=False):
                pe.wait_ge(xn_ready, t + 1)
                if not first:
                    pe.wait_ge(hi_ready, t)
                for h in range(KH):
                    last = nc.tensor.transpose(tr_h[:, h, :], xn[:, buf, h * P:(h + 1) * P], ident[:, :])
                last.then_inc(tr_ready, 1)

            def split_transform(t, buf):
                pe.wait_ge(hi_ready, t + 1)
                pe.wait_ge(lo_ready, t + 1)
                for b in range(4):
                    pe.wait_ge(rel_used, 4 * t + (b + 1))
                    cols = slice(b * 512, (b + 1) * 512)
                    parts = [(a[:, buf, kh, :], w[:, kh, cols]) for kh in range(KH)
                             for a, w in ((x_hi, w_hi), (x_hi, w_lo), (x_lo, w_hi))]
                    for n, (a, w) in enumerate(parts):
                        last = nc.tensor.matmul(rel[b][:, :], a, w, start=(n == 0), stop=(n == len(parts) - 1))
                    last.then_inc(rel_ready, 1)

            def root_product(ps, x_tile):
                for eh in range(KH):
                    for kh in range(KH):
                        last = nc.tensor.matmul(ps[:, eh, :], wroot_sb[:, kh, eh * P:(eh + 1) * P],
                                                x_tile[:, kh, :], start=(kh == 0), stop=(kh == KH - 1))
                return last

            def transform(layer, t):
                pe.wait_ge(xT_ready, TILES * layer + t + 1)
                pe.wait_ge(root_used, TILES * (layer + 1) + t + 2)
                root_product(roots[0], xT).then_inc(root_ready, 1)
                for b in range(4):
                    pe.wait_ge(rel_used, 4 * (TILES * (layer + 1) + t) + (b + 1))
                    for kh in range(KH):
                        last = nc.tensor.matmul(rel[b][:, :], xT[:, kh, :], wrel_sb[:, kh, b * 512:(b + 1) * 512],
                                                start=(kh == 0), stop=(kh == KH - 1))
                    last.then_inc(rel_ready, 1)

            extras = pe.alloc_register("pe_extras")
            pe.reg_mov(extras, 0)

            def products(i):
                for h in range(KH):
                    for j in range(CH):
                        s = (i * CH + j) * D + h * P
                        last = nc.tensor.matmul(seg[i % 2][:, h, :], rows[:, s:s + P], onehot[:, i % 2, j, :],
                                                start=(j == 0), stop=(j == CH - 1))
                return last

            def batches(layer, t):
                first = pe.value_load(batch_row[0:1, ds(t, 1)], min_val=0, max_val=BATCHES)
                end = pe.value_load(batch_row[0:1, ds(t + 1, 1)], min_val=0, max_val=BATCHES)
                with pe.If(end > first):
                    with pe.Fori(first, end) as b:
                        for i in range(RING):
                            pe.wait_ge(onehot_ready, layer * GROUPS + b * RING + (i + 1))
                            pe.wait_ge(gathered[i], (layer * BATCHES + b + 1) * (16 * CH))
                            products(i).then_inc(seg_ready, 1)
                            more = pe.value_load(extra_row[0:1, ds(b * RING + i, 1)], min_val=0, max_val=N // W)
                            with pe.If(more > 0):
                                with pe.Fori(0, more):
                                    pe.wait_ge(onehot_extra, pe.snap(extras, min_val=0, max_val=1 << 20) + 1)
                                    products(i).then_inc(seg_extra, 1)
                                    pe.reg_add(extras, extras, 1)

            pe.wait_ge(ident_ready, 1)
            pe.wait_ge(w_ready, 1)
            for m in range(KH):
                for kh in range(KH):
                    nc.tensor.transpose(rel[m][:, kh * P:(kh + 1) * P], w_raw[:, m, kh * P:(kh + 1) * P], ident[:, :])
                    nc.tensor.transpose(rel[2 + m][:, :].bitcast(bf16)[:, kh * P:(kh + 1) * P],
                                        w_sgn[:, m, kh * P:(kh + 1) * P], ident_bf[:, :])
                last = nc.tensor.matmul(roots[0][:, m, :], ones, diag[:, m, :], start=True, stop=True)
            last.then_inc(w_transposed, 1)

            transposes(0, 0, first=True)
            pe.wait_ge(w_lo_ready, KH)
            pe.wait_ge(w_taken, 1)
            with pe.Fori(0, PAIRS) as i:
                transposes(2 * i + 1, 1)
                split_transform(2 * i, 0)
                transposes(2 * i + 2, 0)
                split_transform(2 * i + 1, 1)
            split_transform(TILES - 1, 0)

            def first_seed(t, buf):
                pe.wait_ge(root_used, t + 1)
                root_product(roots[buf], x_sb[:, ds(t, 1), :].rearrange("p o (h n) -> p (o h) n", h=KH)).then_inc(root_ready, 1)

            pe.wait_ge(root_loaded, 32)
            with pe.Fori(0, PAIRS) as i:
                first_seed(2 * i, 0)
                first_seed(2 * i + 1, 1)
            first_seed(TILES - 1, 0)
            pe.wait_ge(pool_ready, 1)

            with pe.Fori(0, L - 1) as layer:
                pe.wait_ge(rel_loaded, 32 * (layer + 2))
                pe.wait_ge(root_loaded, 32 * (layer + 2))
                pe.sem_inc(pe_mark, 1)
                with pe.Fori(0, TILES) as t:
                    batches(layer, t)
                    transform(layer, t)

            with pe.Fori(0, TILES) as t:
                batches(L - 1, t)
                pe.wait_ge(h_ready, t + 1)
                for h in range(KH):
                    last = nc.tensor.transpose(tr_h[:, h, :], xT[:, h, :], ident[:, :])
                last.then_inc(h_transposed, 1)
                pe.wait_ge(sgn_ready, t + 1)
                for h in range(KH):
                    nc.tensor.transpose(sgn_ps[:, h, :], sgn[:, h * P:(h + 1) * P], ident_bf[:, :])
                pe.wait_ge(mag_ready, t + 1)
                for h in range(KH):
                    last = nc.tensor.transpose(mag_ps[:, h, :], mag[:, h * P:(h + 1) * P], ident[:, :])
                last.then_inc(mag_transposed, 1)
                pe.wait_ge(sgnT_ready, t + 1)
                for h in range(KH):
                    nc.tensor.matmul(lns_sign_ps, sgnT[:, h, :], wsT[:, h, :], start=(h == 0), stop=(h == KH - 1))
                pe.wait_ge(magT_ready, t + 1)
                for h in range(KH):
                    last = nc.tensor.matmul(lns_ps, magT[:, h, :], wT[:, h, :], start=(h == 0), stop=(h == KH - 1))
                last.then_inc(lns_ready, 1)

        @block.scalar
        def _(act):
            def seed(T, t, ps):
                act.wait_ge(root_ready, T + 1)
                act.sem_inc(act_mark, 1)
                for h in range(KH):
                    last = nc.scalar.activation(acc[:, h, ds(t * P, P)], ps[:, h, :], ACT.Identity,
                                                bias=bias_sb[:, h:h + 1])
                last.then_inc(root_used, 1)

            def store(T, t, buf, table, free):
                if free is not None:
                    act.wait_ge(stored[buf], free)
                for b in range(4):
                    act.wait_ge(rel_ready, 4 * T + (b + 1))
                    nc.scalar.copy(stage[:, buf, b * 512:(b + 1) * 512], rel[b][:, :]).then_inc(rel_used, 1)
                act.wait_ge(rel_used, 4 * (T + 2))
                act.dma_start(tables_by_node[table][ds(t * P, P), :], stage[:, buf, :]).then_inc(stored[buf], 16)

            def deviations(lo, hi):
                return nc.scalar.activation(moments[:, lo:hi, 1:2], moments[:, lo:hi, 1:2], ACT.Sqrt, bias=eps_col[:, :])

            def chunk_deviations(c):
                act.wait_ge(var_ready, c + 1)
                deviations(*chunks[c]).then_inc(std_ready, 1)

            def take(t, buf):
                act.wait_ge(tr_ready, t + 1)
                act.sem_inc(act_mark, 1)
                nc.scalar.copy(x_sb[:, ds(t, 1), :].rearrange("p o d -> p (o d)"), tr)
                nc.scalar.copy(x_hi[:, buf, :, :], tr_h).then_inc(hi_ready, 1)

            def pair(i, ahead=None, first=False):
                take(2 * i + 1, 1)
                if ahead is not None:
                    chunk_deviations(ahead)
                store(2 * i, 2 * i, 0, 0, None if first else 16 * i)
                take(2 * i + 2, 0)
                store(2 * i + 1, 2 * i + 1, 1, 0, None if first else 16 * i)

            act.sem_inc(root_used, 2)
            act.sem_inc(rel_used, 4)
            act.wait_ge(rel_loaded, 32)
            for h in range(KH):
                nc.scalar.copy(w_hi[:, h, :], wrel_sb[:, h, :]).then_inc(w_hi_ready, 1)
            act.wait_ge(w_transposed, 1)
            for m in range(KH):
                nc.scalar.copy(wT[:, :, m * P:(m + 1) * P], rel[m][:, 0:D].rearrange("p (h n) -> p h n", h=KH))
                nc.scalar.copy(wsT[:, :, m * P:(m + 1) * P],
                               rel[2 + m][:, :].bitcast(bf16)[:, 0:D].rearrange("p (h n) -> p h n", h=KH))
            nc.scalar.copy(wmax_bc[:, :].rearrange("p (h n) -> p h n", h=KH), roots[0]).then_inc(w_taken, 1)
            act.wait_ge(pads_set, 2)
            chunk_deviations(0)
            take(0, 0)
            pair(0, first=True)
            for c in range(XCHUNKS):
                last_pair = (c + 1) * XC // 2 - 1
                with act.Fori(max(c * XC // 2, 1), last_pair) as i:
                    pair(i)
                pair(last_pair, ahead=c + 1 if c + 1 < XCHUNKS else None)
            store(TILES - 1, TILES - 1, 0, 0, 16 * PAIRS)
            act.wait_ge(root_loaded, 32)
            with act.Fori(0, PAIRS) as i:
                seed(2 * i, 2 * i, roots[0])
                seed(2 * i + 1, 2 * i + 1, roots[1])
            seed(TILES - 1, TILES - 1, roots[0])
            act.wait_ge(pool_ready, 1)

            def rectified(layer, t):
                end = act.value_load(batch_row[0:1, ds(t + 1, 1)], min_val=0, max_val=BATCHES)
                act.wait_ge(group_done, layer * GROUPS + end * RING + RING)
                act.sem_inc(act_mark, 1)
                return nc.scalar.activation(xT[:, :, :], acc[:, :, ds(t * P, P)], ACT.Relu)

            for layer in range(L - 1):
                act.wait_ge(root_loaded, 32 * (layer + 2))
                with act.Fori(0, TILES) as t:
                    rectified(layer, t).then_inc(xT_ready, 1)
                    seed(TILES * (layer + 1) + t, t, roots[0])
                    store(TILES * (layer + 1) + t, t, 0, (layer + 1) % 2, 16 * (PAIRS + 1 + TILES * layer + t))
            with act.Fori(0, TILES) as t:
                rectified(L - 1, t).then_inc(h_ready, 1)
                act.wait_ge(var_ready, t + (XCHUNKS + 1))
                deviations(TILES, TILES + 1).then_inc(std_ready, 1)
                act.wait_ge(z_ready, t + 1)
                nc.scalar.activation(sgn, xn[:, 0, :], ACT.Sign).then_inc(sgn_ready, 1)
                act.wait_ge(mag_transposed, t + 1)
                nc.scalar.copy(magT, mag_ps).then_inc(magT_ready, 1)
                act.wait_ge(lns_ready, t + 1)
                nc.scalar.activation(osgn, lns_sign_ps, ACT.Sign).then_inc(osgn_ready, 1)

        @block.vector
        def _(dve):
            def chained(base, k, ins):
                ins.then_inc(dve_step, 1)
                dve.wait_ge(dve_step, base + k)

            def tile_of(t):
                return x_sb[:, ds(t, 1), :].rearrange("p o d -> p (o d)")

            def pair_stats(t, n, k, last=False):
                for m in range(n):
                    ins = nc.vector.bn_stats(stats[:, m, :], tile_of(t + m))
                ins.then_inc(stats_ready, 1)
                dve.wait_ge(stats_ready, k + 1)
                dve.sem_inc(dve_mark, 1)
                for m in range(n):
                    ins = nc.vector.bn_aggr(tile_moments[:, m, :], stats[:, m, :])
                ins.then_inc(moments_ready, 1)
                dve.wait_ge(moments_ready, k + 1)
                return nc.vector.tensor_copy(moments[:, ds(t, n), :], tile_moments[:, 0:n, :])

            def inverse(lo, hi):
                return nc.vector.reciprocal(moments[:, lo:hi, 1:2], moments[:, lo:hi, 1:2])

            def norm_tile(t, buf, wait=True):
                if wait:
                    dve.wait_ge(tr_ready, t - 1)
                scalars = moments[:, ds(t, 1), :].rearrange("p o a -> p (o a)")
                nc.vector.tensor_scalar(xn[:, buf, :], tile_of(t), scalars[:, 0:1], scalars[:, 1:2],
                                        ALU.subtract, ALU.mult).then_inc(xn_ready, 1)

            nc.vector.memset(x_sb[:, TILES - 1, :], 0.0).then_inc(pads_set, 1)
            nc.vector.memset(eps_col[:, :], LN_EPS).then_inc(pads_set, 1)
            base = 0
            dve.wait_ge(ffn_loaded, 16)
            chained(base, 1, nc.vector.memset(ones, 1.0))
            k = 1
            for h in range(KH):
                chained(base, k + 1, nc.vector.tensor_single_scalar(w_sgn[:, h, :], w_raw[:, h, :], 0.0, ALU.is_lt))
                chained(base, k + 2, nc.vector.scalar_tensor_tensor(w_sgn[:, h, :], w_raw[:, h, :], 0.0, w_sgn[:, h, :], ALU.is_gt, ALU.subtract))
                chained(base, k + 3, nc.vector.scalar_tensor_tensor(mag, w_raw[:, h, :], -1.0, w_raw[:, h, :], ALU.mult, ALU.max))
                chained(base, k + 4, nc.vector.tensor_scalar(w_raw[:, h, :], mag, LOG_EPS, None, ALU.add))
                chained(base, k + 5, nc.vector.reduce_max(wmax[:, h:h + 1], w_raw[:, h, :], AX))
                chained(base, k + 6, nc.vector.reciprocal(wmax[:, 2 + h:3 + h], wmax[:, h:h + 1]))
                chained(base, k + 7, nc.vector.tensor_scalar(w_raw[:, h, :], w_raw[:, h, :], wmax[:, 2 + h:3 + h], None, ALU.mult))
                k += 7
            dve.wait_ge(ident_ready, 1)
            for h in range(KH):
                last = nc.vector.tensor_scalar(diag[:, h, :], ident[:, :], wmax[:, h:h + 1], None, ALU.mult)
            last.then_inc(w_ready, 1)
            base += k

            def group_spans():
                dve.wait_ge(dst_rows_loaded, 16 * 3)
                by_group = dst_rows[0:GROUPS // 2, :].rearrange("p (a e) -> p a e", a=2)
                nc.vector.tensor_reduce(span[0:GROUPS // 2, 0:2], by_group, axis=AX, op=ALU.min)
                nc.vector.tensor_reduce(span[0:GROUPS // 2, 2:4], by_group, axis=AX, op=ALU.max).then_inc(span_ready, 1)

            def passes_and_batches():
                def span_link(k, ins):
                    ins.then_inc(span_step, 1)
                    dve.wait_ge(span_step, k)

                dve.wait_ge(span_loaded, 16 * 3)
                dve.wait_ge(iota_ready, 1)
                nc.vector.tensor_copy(base_row[:, 0:GROUPS], least)
                nc.vector.tensor_copy(base_row[:, GROUPS:GROUPS + 1], least[:, 0:1])
                span_link(1, nc.vector.tensor_tensor(extra_row[:, :], greatest, least, ALU.subtract))
                span_link(2, nc.vector.tensor_single_scalar(extra_row[:, :], extra_row[:, :], W_SHIFT, ALU.arith_shift_right))
                span_link(3, nc.vector.scalar_tensor_tensor(least_by_tile, least_by_tile, tile_end, group_no, ALU.is_lt, ALU.mult))
                span_link(4, nc.vector.reduce_max(need, least_by_tile, AX))
                span_link(5, nc.vector.tensor_scalar(batch_col, need, float(RING - 1), None, ALU.add))
                nc.vector.tensor_single_scalar(batch_col, batch_col, RING.bit_length() - 1, ALU.arith_shift_right).then_inc(batches_ready, 1)

            def keep_low(t, buf):
                dve.wait_ge(hi_ready, t + 1)
                nc.vector.tensor_tensor(x_lo[:, buf, :, :].rearrange("p h n -> p (h n)"), tile_of(t),
                                        x_hi[:, buf, :, :].bitcast(fp32).rearrange("p h n -> p (h n)"),
                                        ALU.subtract).then_inc(lo_ready, 1)

            def pair(i, ahead=None, first=False, stats_ahead=True):
                norm_tile(2 * i + 1, 1, wait=not first)
                keep_low(2 * i, 0)
                if stats_ahead:
                    last = pair_stats(2 * i + XC, 2, i + XC // 2)
                if ahead is not None:
                    if ahead == XCHUNKS - 1:
                        last = pair_stats(TILES - 1, 1, PAIRS)
                    last.then_inc(var_ready, 1)
                    invert_chunk(ahead)
                norm_tile(2 * i + 2, 0, wait=not first)
                keep_low(2 * i + 1, 1)

            def invert_chunk(c):
                dve.wait_ge(std_ready, c + 1)
                inverse(*chunks[c]).then_inc(inv_ready, 1)
                dve.wait_ge(inv_ready, c + 1)

            for h in range(KH):
                dve.wait_ge(w_hi_ready, h + 1)
                nc.vector.tensor_tensor(w_lo[:, h, :], wrel_sb[:, h, :], w_hi[:, h, :].bitcast(fp32),
                                        ALU.subtract).then_inc(w_lo_ready, 1)
            dve.wait_ge(x_loaded[0], 16)
            with dve.Fori(0, XC // 2 - 1) as i:
                pair_stats(2 * i, 2, i)
            pair_stats(XC - 2, 2, XC // 2 - 1).then_inc(var_ready, 1)
            invert_chunk(0)
            norm_tile(0, 0, wait=False)
            dve.wait_ge(x_loaded[1], 16)
            pair(0, first=True)
            for c in range(XCHUNKS):
                more = c + 1 < XCHUNKS
                if c > 0 and more:
                    dve.wait_ge(x_loaded[c + 1], 32 if c + 1 == XCHUNKS - 1 else 16)
                last_pair = (c + 1) * XC // 2 - 1
                if not more:
                    passes_and_batches()
                with dve.Fori(max(c * XC // 2, 1), last_pair) as i:
                    pair(i, stats_ahead=more)
                pair(last_pair, ahead=c + 1 if more else None, stats_ahead=more)
                if c == 1:
                    group_spans()
            keep_low(TILES - 1, 0)
            dve.wait_ge(root_used, TILES + 2)
            nc.vector.memset(acc[:, :, NP_:], 0.0)
            dve.wait_ge(pool_ready, 1)

            extras = dve.alloc_register("dve_extras")
            dve.reg_mov(extras, 0)

            def make_onehot(buf, first_node, g):
                return nc.vector.tensor_tensor(
                    onehot[:, buf, :, :],
                    node_iota[:, ds(first_node, W)].unsqueeze(1).to_broadcast([P, CH, W]),
                    dst_all[:, ds(g * CH, CH)].unsqueeze(2).to_broadcast([P, CH, W]), ALU.is_equal)

            def add(buf, first_node):
                cols = acc[:, :, ds(first_node, W)]
                return nc.vector.tensor_tensor(cols, cols, seg[buf], ALU.add)

            def base_of(g):
                return dve.value_load(base_row[0:1, ds(g, 1)], min_val=0, max_val=N - 1)

            def batch(layer, b):
                for i in range(RING):
                    g = b * RING + i
                    q = layer * GROUPS + g
                    make_onehot((i + 1) % 2, base_of(g + 1), g + 1).then_inc(onehot_ready, 1)
                    first = base_of(g)
                    dve.wait_ge(seg_ready, q + 1)
                    add(i % 2, first).then_inc(acc_added, 1)
                    dve.wait_ge(acc_added, q + 1)
                    more = dve.value_load(extra_row[0:1, ds(g, 1)], min_val=0, max_val=N // W)
                    with dve.If(more > 0):
                        with dve.Fori(1, more + 1) as k:
                            node = nc.s_assert_within(first + k * W, 0, N - 1, skip_runtime_bounds_check_because="k * W is at most the span of the group")
                            done = dve.snap(extras, min_val=0, max_val=1 << 20)
                            make_onehot(i % 2, node, g).then_inc(onehot_extra, 1)
                            dve.wait_ge(seg_extra, done + 1)
                            add(i % 2, node).then_inc(acc_extra, 1)
                            dve.wait_ge(acc_extra, done + 1)
                            dve.reg_add(extras, extras, 1)
                    nc.vector.tensor_copy(idx_ring[:, i, :], idx_all[:, ds((g + RING) * CH, CH)]).then_inc(group_done, 1)

            make_onehot(0, base_of(0), 0).then_inc(onehot_ready, 1)
            with dve.Fori(0, L - 1) as layer:
                with dve.Fori(0, BATCHES) as b:
                    batch(layer, b)
            dve.wait_ge(x_reloaded, 32)
            dve.wait_ge(fbias_loaded, 16)
            with dve.Fori(0, TILES) as t:
                start = dve.value_load(batch_row[0:1, ds(t, 1)], min_val=0, max_val=BATCHES)
                end = dve.value_load(batch_row[0:1, ds(t + 1, 1)], min_val=0, max_val=BATCHES)
                with dve.If(end > start):
                    with dve.Fori(start, end) as b:
                        batch(L - 1, b)
                c = base + t * 7
                dve.wait_ge(h_transposed, t + 1)
                nc.vector.tensor_tensor(x1, tile_of(t), tr, ALU.add).then_inc(x1_ready, 1)
                dve.wait_ge(x1_ready, t + 1)
                nc.vector.bn_stats(stats[:, 0, :], x1).then_inc(stats_ready, 1)
                dve.wait_ge(stats_ready, PAIRS + 2 + t)
                dve.sem_inc(dve_mark, 1)
                nc.vector.bn_aggr(moments[:, TILES, :], stats[:, 0, :]).then_inc(var_ready, 1)
                dve.wait_ge(std_ready, t + (XCHUNKS + 1))
                inverse(TILES, TILES + 1).then_inc(inv_ready, 1)
                dve.wait_ge(inv_ready, t + (XCHUNKS + 1))
                nc.vector.tensor_scalar(xn[:, 0, :], x1, moments[:, TILES, 0:1], moments[:, TILES, 1:2],
                                        ALU.subtract, ALU.mult).then_inc(z_ready, 1)
                dve.wait_ge(z_ready, t + 1)
                chained(c, 1, nc.vector.scalar_tensor_tensor(mag, xn[:, 0, :], -1.0, xn[:, 0, :], ALU.mult, ALU.max))
                chained(c, 2, nc.vector.tensor_scalar(mag, mag, LOG_EPS, None, ALU.add))
                chained(c, 3, nc.vector.reduce_max(mmax[:, 0:1], mag, AX))
                chained(c, 4, nc.vector.reciprocal(mmax[:, 1:2], mmax[:, 0:1]))
                nc.vector.tensor_scalar(mag, mag, mmax[:, 1:2], None, ALU.mult).then_inc(mag_ready, 1)
                chained(c, 5, nc.vector.tensor_tensor(x1, x1, fbias_bc[:, :], ALU.add))
                dve.wait_ge(mag_transposed, t + 1)
                nc.vector.tensor_copy(sgnT, sgn_ps).then_inc(sgnT_ready, 1)
                dve.wait_ge(lns_ready, t + 1)
                chained(c, 6, nc.vector.scalar_tensor_tensor(mag, lns_ps, mmax[:, 0:1], wmax_bc[:, :], ALU.mult, ALU.mult))
                dve.wait_ge(osgn_ready, t + 1)
                chained(c, 7, nc.vector.tensor_tensor(mag, mag, osgn, ALU.mult))
                nc.vector.tensor_tensor(tile_of(t), mag, x1, ALU.add).then_inc(out_ready, 1)
                dve.wait_ge(out_ready, t + 1)


_INS = ["x", "src", "dst", "edge_type_8", "L0_gnn_W_rel", "L0_gnn_W_root", "L0_gnn_bias", "L0_ffn_weight", "L0_ffn_bias"]
_OUTS = [((N, D), "float32")]


def kernel(**inputs):
    import numpy as _np
    import concourse.bacc as _bacc
    from concourse import mybir as _mybir
    from concourse.bass_utils import run_bass_kernel_spmd as _run

    nc = _bacc.Bacc("TRN2", target_bir_lowering=False, num_devices=1)
    arrays, args = {}, []
    for name in _INS:
        a = _np.ascontiguousarray(inputs[name])
        arrays[f"in_{name}_dram"] = a
        args.append(nc.dram_tensor(f"in_{name}_dram", a.shape, _mybir.dt.from_np(a.dtype), kind="ExternalInput").ap())
    for i, (shape, dtype) in enumerate(_OUTS):
        dt = _mybir.dt.from_np(_np.dtype(dtype))
        args.append(nc.dram_tensor(f"out_{i}_dram", shape, dt, kind="ExternalOutput").ap())
    gnn_ffn(nc, *args)
    r = _run(nc, [arrays], core_ids=[0])
    got = tuple(r.results[0][f"out_{i}_dram"] for i in range(len(_OUTS)))
    return got[0]
```

```python
from contextlib import ExitStack

import concourse.bass as bass
from concourse import mybir

N, D, E, R, L = 6250, 256, 200000, 8, 3
P = 128
P_SHIFT = P.bit_length() - 1
KH = D // P
TILES = -(-N // P)
PAIRS = TILES // 2
LAST_ROWS = N - (TILES - 1) * P
NP_ = TILES * P
CH = 8
GE = CH * P
GROUPS = -(-E // GE)
FULL = E // GE
TAIL = E - FULL * GE
TAIL_CH = -(-TAIL // P)
RING = 4
BATCHES = GROUPS // RING
NO_NODE = 1 << 14
XC = 6
XCHUNKS = 8
EDGE_PIECES = 4
LN_EPS = 1e-5
LOG_EPS = 1e-8
assert TILES == XC * XCHUNKS + 1 and XC % 2 == 0 and 0 < TAIL_CH < CH and GROUPS % RING == 0 and TILES % 2 == 1
assert NP_ < NO_NODE and NP_ * R < 1 << 16


def gnn_ffn(nc, x, src, dst, etype, w_rel, w_root, gnn_bias, ffn_w, ffn_b, out):
    fp32, bf16 = mybir.dt.float32, mybir.dt.bfloat16
    f32r = mybir.dt.float32r
    i32, u32, i16, u16 = mybir.dt.int32, mybir.dt.uint32, mybir.dt.int16, mybir.dt.uint16
    ALU = mybir.AluOpType
    ACT = mybir.ActivationFunctionType
    AX = mybir.AxisListType.X
    ds = bass.ds

    tables = [nc.dram_tensor(f"message_table{i}", [NP_ * R, D], fp32, kind="Internal").ap() for i in range(2)]
    span_dram = nc.dram_tensor("group_span", [2, GROUPS], fp32, kind="Internal").ap()
    batch_dram = nc.dram_tensor("tile_batches", [1, TILES], i32, kind="Internal").ap()
    tables_by_node = [table.rearrange("(n r) e -> n (r e)", r=R) for table in tables]

    ctx = ExitStack()
    with ctx:
        def sb(name, shape, dt):
            return ctx.enter_context(nc.sbuf_tensor(name, shape, dt))

        def pb(name, shape, dt=fp32):
            return ctx.enter_context(nc.psum_tensor(name, shape, dt))

        def sem(name):
            return ctx.enter_context(nc.semaphore(name))

        x_sb = sb("x_sb", [P, TILES, D], fp32)
        arena = nc.sbuf_base
        acc = sb("acc", [P, TILES + 1, D], fp32)
        def in_arena(name, shape, at_bytes):
            return nc.alloc_sbuf_tensor_at(name, shape, f32r, offset=arena + at_bytes)

        w_hi = in_arena("w_hi", [P, KH, R * D], 0)
        w_lo = in_arena("w_lo", [P, KH, R * D], 4 * KH * R * D)
        x_hi = in_arena("x_hi", [P, 2, KH, P], 8 * KH * R * D)
        x_lo = in_arena("x_lo", [P, 2, KH, P], 8 * KH * R * D + 8 * KH * P)
        ARENA_TILES = -(-(8 * KH * R * D + 16 * KH * P) // (4 * D))
        wrel_sb = sb("wrel_sb", [P, KH, R * D], fp32)
        wroot_sb = sb("wroot_sb", [P, KH, D], fp32)
        bias_cols = sb("bias_cols", [P, L - 1, KH], fp32)
        rows = sb("rows", [P, RING * CH * D], fp32)
        stage = sb("stage", [P, 2, R * D], fp32)
        idx_all = sb("idx_all", [P, (GROUPS + RING) * CH], u16)
        dst_all = sb("dst_all", [P, (GROUPS + 1) * CH], i16)
        dst_mod = sb("dst_mod", [P, (GROUPS + 1) * CH], i16)
        in_first = sb("in_first", [P, GROUPS], fp32)
        in_second = sb("in_second", [P, GROUPS], fp32)
        own_place = sb("own_place", [P, 1], fp32)
        node_iota = sb("node_iota", [P, NP_], i16)
        idx_ring = sb("idx_ring", [P, RING, CH], u32)
        onehot = sb("onehot", [P, 2, CH, P], fp32)
        xT = sb("xT", [P, KH, P], fp32)
        xn = sb("xn", [P, 2, D], fp32)
        ident = sb("ident", [P, P], fp32)
        ident_bf = sb("ident_bf", [P, P], bf16)
        stats = sb("stats", [P, 2, 6], fp32)
        moments = sb("moments", [P, TILES + 1, 2], fp32)
        tile_moments = sb("tile_moments", [P, 2, 2], fp32)
        eps_col = sb("eps_col", [P, 1], fp32)
        base_row = sb("base_row", [1, GROUPS], i32)
        extra_row = sb("extra_row", [1, GROUPS], i32)
        batch_row = sb("batch_row", [1, TILES + 1], i32)
        wT = sb("wT", [P, KH, D], fp32)
        wsT = sb("wsT", [P, KH, D], bf16)
        wmax_bc = sb("wmax_bc", [P, D], fp32)
        wmax = sb("wmax", [P, 4], fp32)
        spare = stage[:, 1, :]
        x1, mag, osgn = spare[:, 0:D], spare[:, D:2 * D], spare[:, 2 * D:3 * D]
        magT = spare[:, 3 * D:4 * D].rearrange("p (h n) -> p h n", h=KH)
        sgn = spare[:, 4 * D:4 * D + P].bitcast(bf16)
        sgnT = spare[:, 4 * D + P:5 * D].bitcast(bf16).rearrange("p (h n) -> p h n", h=KH)
        first_wroot = spare[:, 0:KH * D].rearrange("p (h e) -> p h e", h=KH)
        bias_bc, fbias_bc = spare[:, 5 * D:6 * D], spare[:, 6 * D:7 * D]
        mmax = sb("mmax", [P, 2], fp32)

        CW = GROUPS * CH
        raw = rows[:, :].bitcast(i32)
        src_raw, type_raw, dst_raw = raw[:, 0:CW], raw[:, CW:2 * CW], raw[:, 2 * CW:3 * CW]
        dst_rows = raw[:, 3 * CW:3 * CW + 2 * GE]
        at = 3 * CW + 2 * GE
        span = rows[:, at:at + 4]
        at += 4
        least, greatest = rows[:, at:at + GROUPS], rows[:, at + GROUPS:at + 2 * GROUPS]
        at += 2 * GROUPS
        narrow = rows[:, at:at + GROUPS]
        least_place = raw[:, at + GROUPS:at + 2 * GROUPS]
        at += 2 * GROUPS
        least_by_tile = rows[0:TILES, at:at + GROUPS]
        tile_end, tile_pace = rows[0:TILES, at + GROUPS:at + GROUPS + 1], rows[0:TILES, at + GROUPS + 3:at + GROUPS + 4]
        need = rows[0:TILES, at + GROUPS + 1:at + GROUPS + 2]
        batch_col = raw[0:TILES, at + GROUPS + 2:at + GROUPS + 3]
        group_no = node_iota[0:TILES, 1:GROUPS + 1]
        w_raw = onehot[:, :, :, :].rearrange("p a c n -> p (a c n)")[:, 0:KH * D].rearrange("p (h k) -> p h k", h=KH)
        w_sgn = spare[:, 3 * D:4 * D].bitcast(bf16).rearrange("p (h k) -> p h k", h=KH)
        ones = x1[:, 0:P]
        diag = mag[:, :].rearrange("p (h n) -> p h n", h=KH)

        banks = [pb(f"bank{i}", [P, 512]) for i in range(8)]
        seg = [banks[i][:, 0:D] for i in range(2)]
        rel = banks[2:6]
        root_ps = banks[6][:, 0:D]
        tr = banks[7][:, 0:D]
        tr_h = tr.rearrange("p (h n) -> p h n", h=KH)
        mag_ps = rel[0][:, 0:D].rearrange("p (h n) -> p h n", h=KH)
        sgn_ps = rel[1][:, :].bitcast(bf16)[:, 0:D].rearrange("p (h n) -> p h n", h=KH)
        lns_ps = rel[2][:, 0:D]
        lns_sign_ps = rel[3][:, 0:D]

        x_loaded = [sem(f"x_loaded{c}") for c in range(XCHUNKS)]
        x_reloaded = sem("x_reloaded")
        pads_set = sem("pads_set")
        edges_loaded = sem("edges_loaded")
        tail_loaded = sem("tail_loaded")
        setup = sem("setup")
        dst_rows_loaded = sem("dst_rows_loaded")
        span_ready = sem("span_ready")
        span_stored = sem("span_stored")
        span_loaded = sem("span_loaded")
        span_step = sem("span_step")
        batches_ready = sem("batches_ready")
        batches_stored = sem("batches_stored")
        batches_loaded = sem("batches_loaded")
        dst_ready = sem("dst_ready")
        pool_ready = sem("pool_ready")
        acc_cleared = sem("acc_cleared")
        ident_ready = sem("ident_ready")
        iota_ready = sem("iota_ready")
        rel_loaded = sem("rel_loaded")
        first_root_loaded = sem("first_root_loaded")
        root_loaded = sem("root_loaded")
        w_hi_ready = sem("w_hi_ready")
        w_lo_ready = sem("w_lo_ready")
        ffn_loaded = sem("ffn_loaded")
        bias_cols_loaded = sem("bias_cols_loaded")
        biases_loaded = sem("biases_loaded")
        w_ready = sem("w_ready")
        w_transposed = sem("w_transposed")
        w_taken = sem("w_taken")
        stats_ready = sem("stats_ready")
        moments_ready = sem("moments_ready")
        var_ready = sem("var_ready")
        std_ready = sem("std_ready")
        inv_ready = sem("inv_ready")
        xn_ready = sem("xn_ready")
        tr_ready = sem("tr_ready")
        xT_ready = sem("xT_ready")
        sums_taken = sem("sums_taken")
        root_ready = sem("root_ready")
        root_used = sem("root_used")
        rel_ready = sem("rel_ready")
        rel_used = sem("rel_used")
        stored = [sem("stored0"), sem("stored1")]
        hi_ready = sem("hi_ready")
        lo_ready = sem("lo_ready")
        gathered = [sem(f"gathered{i}") for i in range(RING)]
        rest_gathered = sem("rest_gathered")
        onehot_ready = sem("onehot_ready")
        seg_ready = sem("seg_ready")
        acc_added = sem("acc_added")
        onehot_extra = sem("onehot_extra")
        seg_extra = sem("seg_extra")
        acc_extra = sem("acc_extra")
        group_done = sem("group_done")
        dve_mark, act_mark = sem("dve_mark"), sem("act_mark")
        pool_mark, pe_mark = sem("pool_mark"), sem("pe_mark")
        x1_ready = sem("x1_ready")
        dve_step = sem("dve_step")
        z_ready = sem("z_ready")
        mag_ready = sem("mag_ready")
        sgn_ready = sem("sgn_ready")
        mag_transposed = sem("mag_transposed")
        magT_ready = sem("magT_ready")
        sgnT_ready = sem("sgnT_ready")
        lns_ready = sem("lns_ready")
        osgn_ready = sem("osgn_ready")
        out_ready = sem("out_ready")
        out_stored = sem("out_stored")

        chunks = [(c * XC, (c + 1) * XC) for c in range(XCHUNKS - 1)] + [((XCHUNKS - 1) * XC, TILES)]
        x_full = x[0:(TILES - 1) * P, :].rearrange("(t p) d -> p t d", p=P)

        block = ctx.enter_context(nc.Block())

        @block.sync
        def _(sp):
            def load_rel(l):
                for h in range(KH):
                    sp.dma_start(
                        wrel_sb[:, h, :].rearrange("p (r e) -> p r e", r=R),
                        w_rel[ds(l, 1), :, h * P:(h + 1) * P, :].rearrange("o r p e -> (o p) r e"),
                    ).then_inc(rel_loaded, 16)

            def load_root(l, to, loaded):
                sp.dma_start(to, w_root[ds(l, 1), :, :].rearrange("o (h p) e -> (o p) h e", p=P)).then_inc(loaded, 16)

            sp.dma_start(w_raw, ffn_w.rearrange("(h p) k -> p h k", p=P)).then_inc(ffn_loaded, 16)
            load_rel(0)
            for c, (lo, hi) in enumerate(chunks):
                end = min(hi, TILES - 1)
                sp.dma_start(x_sb[:, lo:end, :], x_full[:, lo:end, :]).then_inc(x_loaded[c], 16)
            sp.wait_ge(pads_set, 1)
            sp.dma_start(x_sb[0:LAST_ROWS, TILES - 1, :], x[(TILES - 1) * P:N, :]).then_inc(x_loaded[-1], 16)
            with nc.allow_non_contiguous_dma(reason="one bias value to a partition, half and layer"):
                sp.dma_start(bias_cols[:, :, :],
                             gnn_bias[0:L - 1, :].rearrange("l (h p) -> p l h", p=P)).then_inc(bias_cols_loaded, 16)
            load_root(1, wroot_sb[:, :, :], root_loaded)
            pieces = [(a * FULL // EDGE_PIECES, (a + 1) * FULL // EDGE_PIECES) for a in range(EDGE_PIECES)]
            for n, (a, b) in enumerate(pieces):
                for m, (to, of) in enumerate(((dst_raw, dst), (src_raw, src), (type_raw, etype))):
                    sp.wait_ge(rel_used, 8 * (3 * n + m + 1))
                    sp.dma_start(to[:, a * CH:b * CH].rearrange("p (g j) -> p g j", j=CH),
                                 of[a * GE:b * GE].rearrange("(g p j) -> p g j", p=P, j=CH)).then_inc(edges_loaded, 16)
            sp.wait_ge(w_lo_ready, KH)
            load_rel(1)
            sp.wait_ge(stored[1], 16 * PAIRS)
            load_root(0, first_wroot, first_root_loaded)
            sp.dma_start(bias_bc, gnn_bias[L - 1:L, :].to_broadcast([P, D])).then_inc(biases_loaded, 16)
            sp.dma_start(fbias_bc, ffn_b.unsqueeze(0).to_broadcast([P, D])).then_inc(biases_loaded, 16)
            sp.wait_ge(rel_used, 4 * (2 * TILES + 1))
            load_rel(2)
            sp.wait_ge(root_used, TILES + 1)
            load_root(2, wroot_sb[:, :, :], root_loaded)
            sp.dma_start(x_sb[:, 0:TILES - 1, :], x_full).then_inc(x_reloaded, 16)
            sp.dma_start(x_sb[0:LAST_ROWS, TILES - 1, :], x[(TILES - 1) * P:N, :]).then_inc(x_reloaded, 16)
            with sp.Fori(0, TILES - 1) as t:
                sp.wait_ge(out_ready, t + 1)
                sp.dma_start(out[ds(t * P, P), :],
                             x_sb[:, ds(t, 1), :].rearrange("p o d -> p (o d)")).then_inc(out_stored, 16)
            sp.wait_ge(out_ready, TILES)
            sp.dma_start(out[(TILES - 1) * P:N, :], x_sb[0:LAST_ROWS, TILES - 1, :]).then_inc(out_stored, 16)
            sp.wait_ge(out_stored, 16 * TILES)

        @block.gpsimd
        def _(pool):
            count = [0]

            def step(ins):
                count[0] += 1
                ins.then_inc(setup, 1)
                pool.wait_ge(setup, count[0])

            step(pool.memset(ident[:, :], 1.0))
            step(pool.affine_select(ident[:, :], ident[:, :], pattern=[[1, P]], compare_op=ALU.is_equal,
                                    fill=0.0, base=0, channel_multiplier=-1))
            pool.tensor_copy(ident_bf[:, :], ident[:, :]).then_inc(ident_ready, 1)
            pad = slice(FULL * CH, CW)
            pool.memset(src_raw[:, pad], 0)
            pool.memset(type_raw[:, pad], 0)
            step(pool.memset(dst_raw[:, pad], NO_NODE))
            full = FULL * GE
            for to, of in ((src_raw, src), (type_raw, etype), (dst_raw, dst)):
                for j in range(TAIL_CH):
                    n = min(P, TAIL - j * P)
                    pool.dma_start(to[0:n, FULL * CH + j:FULL * CH + j + 1],
                                   of[full + j * P:full + j * P + n].unsqueeze(1)).then_inc(tail_loaded, 16)
            half = GROUPS // 2
            pool.dma_start(dst_rows[0:half - 1, :],
                           dst[0:(half - 1) * 2 * GE].rearrange("(p e) -> p e", p=half - 1)).then_inc(dst_rows_loaded, 16)
            pool.dma_start(dst_rows[half - 1:half, 0:GE], dst[(FULL - 1) * GE:full].unsqueeze(0)).then_inc(dst_rows_loaded, 16)
            pool.dma_start(dst_rows[half - 1:half, GE:2 * GE], dst[E - GE:E].unsqueeze(0)).then_inc(dst_rows_loaded, 16)
            step(pool.iota(node_iota[:, :], pattern=[[1, NP_]], base=0, channel_multiplier=0))
            step(pool.iota(batch_col, pattern=[[0, 1]], base=P, channel_multiplier=P))
            step(pool.tensor_copy(tile_end, batch_col))
            step(pool.iota(batch_col, pattern=[[0, 1]], base=2 * RING, channel_multiplier=RING))
            step(pool.tensor_copy(tile_pace, batch_col))
            step(pool.iota(least_place[:, 0:1], pattern=[[0, 1]], base=0, channel_multiplier=1))
            pool.tensor_copy(own_place[:, :], least_place[:, 0:1]).then_inc(iota_ready, 1)
            pool.wait_ge(edges_loaded, 16 * 3 * EDGE_PIECES)
            pool.wait_ge(tail_loaded, 16 * 3 * TAIL_CH)
            step(pool.tensor_scalar(src_raw, src_raw, float(R), None, ALU.mult))
            step(pool.tensor_tensor(src_raw, src_raw, type_raw, ALU.add))
            step(pool.tensor_copy(idx_all[:, 0:CW], src_raw))
            step(pool.tensor_copy(idx_all[:, CW:], idx_all[:, 0:RING * CH]))
            step(pool.tensor_copy(dst_all[:, 0:CW], dst_raw))
            step(pool.tensor_copy(dst_all[:, CW:CW + CH], dst_raw[:, 0:CH]))
            pool.sem_inc(dst_ready, 1)
            step(pool.tensor_copy(idx_ring[:, :, :].rearrange("p i j -> p (i j)"), idx_all[:, 0:RING * CH]))
            half = GROUPS // 2
            pool.wait_ge(span_ready, 1)
            for m in range(2):
                pool.dma_start(span_dram[m, :].rearrange("(p a) -> p a", a=2),
                               span[0:half, 2 * m:2 * m + 2]).then_inc(span_stored, 16)
            pool.wait_ge(span_stored, 32)
            pool.dma_start(least, span_dram[0:1, :].to_broadcast([P, GROUPS])).then_inc(span_loaded, 16)
            pool.dma_start(greatest, span_dram[1:2, :].to_broadcast([P, GROUPS])).then_inc(span_loaded, 16)
            step(pool.memset(batch_row[:, 0:1], 0))
            pool.wait_ge(batches_ready, 1)
            pool.dma_start(batch_dram[0, :].unsqueeze(1), batch_col).then_inc(batches_stored, 16)
            pool.wait_ge(batches_stored, 16)
            pool.dma_start(batch_row[:, 1:TILES + 1], batch_dram[0:1, :]).then_inc(batches_loaded, 16)
            pool.wait_ge(batches_loaded, 16)
            pool.sem_inc(pool_ready, 1)
            pool.sem_inc(group_done, RING)

            for layer in range(L):
                pool.wait_ge(stored[0], 16 * (PAIRS + 1 + TILES * layer))
                if layer == 0:
                    pool.wait_ge(stored[1], 16 * PAIRS)
                pool.sem_inc(pool_mark, 1)
                def gather_batch(b, last=False):
                    for i in range(RING):
                        pool.wait_ge(group_done, layer * GROUPS + b * RING + (i + 1))
                        pool.sem_inc(pool_mark, 1)
                        n = TAIL_CH if last and i == RING - 1 else CH
                        for j in range(n):
                            s = (i * CH + j) * D
                            pool.indirect_dma_start(
                                rows[:, s:s + D], None, tables[layer % 2],
                                bass.IndirectOffsetOnAxis(ap=idx_ring[:, i, j:j + 1], axis=0),
                            ).then_inc(gathered[i] if i < RING - 1 or j < TAIL_CH else rest_gathered, 16)

                with pool.Fori(0, BATCHES - 1) as b:
                    gather_batch(b)
                gather_batch(BATCHES - 1, last=True)

        @block.tensor
        def _(pe):
            def transposes(t, buf, first=False):
                pe.wait_ge(xn_ready, t + 1)
                if not first:
                    pe.wait_ge(hi_ready, t)
                for h in range(KH):
                    last = nc.tensor.transpose(tr_h[:, h, :], xn[:, buf, h * P:(h + 1) * P], ident[:, :])
                last.then_inc(tr_ready, 1)

            def split_transform(t, buf):
                pe.wait_ge(hi_ready, t + 1)
                pe.wait_ge(lo_ready, t + 1)
                for b in range(4):
                    pe.wait_ge(rel_used, 4 * t + (b + 1))
                    cols = slice(b * 512, (b + 1) * 512)
                    parts = [(a[:, buf, kh, :], w[:, kh, cols]) for kh in range(KH)
                             for a, w in ((x_hi, w_hi), (x_hi, w_lo), (x_lo, w_hi))]
                    for n, (a, w) in enumerate(parts):
                        last = nc.tensor.matmul(rel[b][:, :], a, w, start=(n == 0), stop=(n == len(parts) - 1))
                    last.then_inc(rel_ready, 1)

            def transposed_sums(layer, t):
                for h in range(KH):
                    if layer == 0:
                        x_tile = x_sb[:, ds(t, 1), :].rearrange("p o (h n) -> p (o h) n", h=KH)
                        for kh in range(KH):
                            nc.tensor.matmul(tr_h[:, h, :], first_wroot[:, kh, h * P:(h + 1) * P], x_tile[:, kh, :],
                                             start=(kh == 0), stop=False)
                    if h == 0:
                        pe.wait_ge(sums_taken, TILES * layer + t + 1)
                        pe.sem_inc(pe_mark, 1)
                    if layer == 0:
                        last = nc.tensor.matmul(tr_h[:, h, :], xn[:, 0, h * P:(h + 1) * P], ident[:, :],
                                                start=False, stop=True)
                    else:
                        last = nc.tensor.transpose(tr_h[:, h, :], xn[:, 0, h * P:(h + 1) * P], ident[:, :])
                return last

            def transform(layer, t):
                transposed_sums(layer, t).then_inc(tr_ready, 1)
                pe.wait_ge(xT_ready, TILES * layer + t + 1)
                for b in range(4):
                    pe.wait_ge(rel_used, 4 * (TILES * (layer + 1) + t) + (b + 1))
                    for kh in range(KH):
                        last = nc.tensor.matmul(rel[b][:, :], xT[:, kh, :], wrel_sb[:, kh, b * 512:(b + 1) * 512],
                                                start=(kh == 0), stop=(kh == KH - 1))
                    last.then_inc(rel_ready, 1)
                pe.wait_ge(root_used, TILES * layer + t + 1)
                for kh in range(KH):
                    last = nc.tensor.matmul(root_ps, xT[:, kh, :], wroot_sb[:, kh, :], start=(kh == 0), stop=(kh == KH - 1))
                last.then_inc(root_ready, 1)

            extras = pe.alloc_register("pe_extras")
            pe.reg_mov(extras, 0)

            def products(i):
                for j in range(CH):
                    s = (i * CH + j) * D
                    last = nc.tensor.matmul(seg[i % 2], onehot[:, i % 2, j, :], rows[:, s:s + D],
                                            start=(j == 0), stop=(j == CH - 1))
                return last

            def batches(layer, t):
                first = pe.value_load(batch_row[0:1, ds(t, 1)], min_val=0, max_val=BATCHES)
                end = pe.value_load(batch_row[0:1, ds(t + 1, 1)], min_val=0, max_val=BATCHES)
                with pe.If(end > first):
                    with pe.Fori(first, end) as b:
                        for i in range(RING):
                            pe.wait_ge(onehot_ready, layer * GROUPS + b * RING + (i + 1))
                            if i < RING - 1:
                                pe.wait_ge(gathered[i], (layer * BATCHES + b + 1) * (16 * CH))
                            else:
                                pe.wait_ge(gathered[i], (layer * BATCHES + b + 1) * (16 * TAIL_CH))
                                pe.sem_inc(pe_mark, 1)
                                with pe.If(b < BATCHES - 1):
                                    pe.wait_ge(rest_gathered, (layer * (BATCHES - 1) + b + 1) * (16 * (CH - TAIL_CH)))
                                    pe.sem_inc(pe_mark, 1)
                            products(i).then_inc(seg_ready, 1)
                            more = pe.value_load(extra_row[0:1, ds(b * RING + i, 1)], min_val=0, max_val=TILES)
                            with pe.If(more > 0):
                                with pe.Fori(0, more):
                                    pe.wait_ge(onehot_extra, pe.snap(extras, min_val=0, max_val=1 << 20) + 1)
                                    products(i).then_inc(seg_extra, 1)
                                    pe.reg_add(extras, extras, 1)

            pe.wait_ge(ident_ready, 1)
            pe.wait_ge(w_ready, 1)
            for m in range(KH):
                for kh in range(KH):
                    nc.tensor.transpose(rel[m][:, kh * P:(kh + 1) * P], w_raw[:, m, kh * P:(kh + 1) * P], ident[:, :])
                    nc.tensor.transpose(rel[2 + m][:, :].bitcast(bf16)[:, kh * P:(kh + 1) * P],
                                        w_sgn[:, m, kh * P:(kh + 1) * P], ident_bf[:, :])
                last = nc.tensor.matmul(root_ps[:, m * P:(m + 1) * P], ones, diag[:, m, :], start=True, stop=True)
            last.then_inc(w_transposed, 1)

            transposes(0, 0, first=True)
            pe.wait_ge(w_lo_ready, KH)
            pe.wait_ge(w_taken, 1)
            with pe.Fori(0, PAIRS) as i:
                transposes(2 * i + 1, 1)
                split_transform(2 * i, 0)
                transposes(2 * i + 2, 0)
                split_transform(2 * i + 1, 1)
            split_transform(TILES - 1, 0)

            pe.wait_ge(pool_ready, 1)

            for layer in range(L - 1):
                with pe.Fori(0, TILES) as t:
                    batches(layer, t)
                    if layer == 0:
                        pe.wait_ge(first_root_loaded, 16)
                    pe.wait_ge(rel_loaded, 32 * (layer + 2))
                    pe.wait_ge(root_loaded, 16 * (layer + 1))
                    transform(layer, t)

            with pe.Fori(0, TILES) as t:
                batches(L - 1, t)
                pe.wait_ge(sgn_ready, t + 1)
                for h in range(KH):
                    nc.tensor.transpose(sgn_ps[:, h, :], sgn[:, h * P:(h + 1) * P], ident_bf[:, :])
                pe.wait_ge(mag_ready, t + 1)
                for h in range(KH):
                    last = nc.tensor.transpose(mag_ps[:, h, :], mag[:, h * P:(h + 1) * P], ident[:, :])
                last.then_inc(mag_transposed, 1)
                pe.wait_ge(sgnT_ready, t + 1)
                for h in range(KH):
                    nc.tensor.matmul(lns_sign_ps, sgnT[:, h, :], wsT[:, h, :], start=(h == 0), stop=(h == KH - 1))
                pe.wait_ge(magT_ready, t + 1)
                for h in range(KH):
                    last = nc.tensor.matmul(lns_ps, magT[:, h, :], wT[:, h, :], start=(h == 0), stop=(h == KH - 1))
                last.then_inc(lns_ready, 1)

        @block.scalar
        def _(act):
            def sums_of(t):
                return acc[:, ds(t, 1), :].rearrange("p o d -> p (o d)")

            def seed(T, t):
                act.wait_ge(root_ready, T + 1)
                act.sem_inc(act_mark, 1)
                nc.scalar.copy(sums_of(t), root_ps).then_inc(root_used, 1)

            def store(T, t, buf, table, free):
                if free is not None:
                    act.wait_ge(stored[buf], free)
                for b in range(4):
                    act.wait_ge(rel_ready, 4 * T + (b + 1))
                    nc.scalar.copy(stage[:, buf, b * 512:(b + 1) * 512], rel[b][:, :]).then_inc(rel_used, 1)
                act.wait_ge(rel_used, 4 * (T + 2))
                act.dma_start(tables_by_node[table][ds(t * P, P), :], stage[:, buf, :]).then_inc(stored[buf], 16)

            def deviations(lo, hi):
                return nc.scalar.activation(moments[:, lo:hi, 1:2], moments[:, lo:hi, 1:2], ACT.Sqrt, bias=eps_col[:, :])

            def chunk_deviations(c):
                act.wait_ge(var_ready, c + 1)
                deviations(*chunks[c]).then_inc(std_ready, 1)

            def take(t, buf):
                act.wait_ge(tr_ready, t + 1)
                act.sem_inc(act_mark, 1)
                nc.scalar.copy(x_sb[:, ds(t, 1), :].rearrange("p o d -> p (o d)"), tr)
                nc.scalar.copy(x_hi[:, buf, :, :], tr_h).then_inc(hi_ready, 1)

            def pair(i, ahead=None, first=False):
                take(2 * i + 1, 1)
                if ahead is not None:
                    chunk_deviations(ahead)
                store(2 * i, 2 * i, 0, 0, None if first else 16 * i)
                take(2 * i + 2, 0)
                store(2 * i + 1, 2 * i + 1, 1, 0, None if first else 16 * i)

            act.sem_inc(root_used, 1)
            act.sem_inc(rel_used, 4)
            act.wait_ge(rel_loaded, 32)
            for h in range(KH):
                nc.scalar.copy(w_hi[:, h, :], wrel_sb[:, h, :]).then_inc(w_hi_ready, 1)
            act.wait_ge(w_transposed, 1)
            for m in range(KH):
                nc.scalar.copy(wT[:, :, m * P:(m + 1) * P], rel[m][:, 0:D].rearrange("p (h n) -> p h n", h=KH))
                nc.scalar.copy(wsT[:, :, m * P:(m + 1) * P],
                               rel[2 + m][:, :].bitcast(bf16)[:, 0:D].rearrange("p (h n) -> p h n", h=KH))
            nc.scalar.copy(wmax_bc[:, :], root_ps).then_inc(w_taken, 1)
            act.wait_ge(pads_set, 2)
            chunk_deviations(0)
            take(0, 0)
            pair(0, first=True)
            for c in range(XCHUNKS):
                last_pair = (c + 1) * XC // 2 - 1
                with act.Fori(max(c * XC // 2, 1), last_pair) as i:
                    pair(i)
                pair(last_pair, ahead=c + 1 if c + 1 < XCHUNKS else None)
            store(TILES - 1, TILES - 1, 0, 0, 16 * PAIRS)
            act.wait_ge(pool_ready, 1)
            act.wait_ge(bias_cols_loaded, 16)
            for layer in range(L - 1):
                with act.Fori(0, TILES) as t:
                    T = TILES * (layer + 1) + t
                    end = act.value_load(batch_row[0:1, ds(t + 1, 1)], min_val=0, max_val=BATCHES)
                    act.wait_ge(group_done, layer * GROUPS + end * RING + RING)
                    act.sem_inc(act_mark, 1)
                    nc.scalar.copy(xn[:, 0, :], sums_of(t)).then_inc(sums_taken, 1)
                    act.wait_ge(tr_ready, T + 1)
                    act.sem_inc(act_mark, 1)
                    for h in range(KH):
                        last = nc.scalar.activation(xT[:, h, :], tr_h[:, h, :], ACT.Relu,
                                                    bias=bias_cols[:, layer, h:h + 1])
                    last.then_inc(xT_ready, 1)
                    store(T, t, 0, (layer + 1) % 2, 16 * (PAIRS + 1 + TILES * layer + t))
                    seed(TILES * layer + t, t)
            with act.Fori(0, TILES) as t:
                act.wait_ge(var_ready, t + (XCHUNKS + 1))
                deviations(TILES, TILES + 1).then_inc(std_ready, 1)
                act.wait_ge(z_ready, t + 1)
                nc.scalar.activation(sgn, xn[:, 0, :], ACT.Sign).then_inc(sgn_ready, 1)
                act.wait_ge(mag_transposed, t + 1)
                nc.scalar.copy(magT, mag_ps).then_inc(magT_ready, 1)
                act.wait_ge(lns_ready, t + 1)
                nc.scalar.activation(osgn, lns_sign_ps, ACT.Sign).then_inc(osgn_ready, 1)

        @block.vector
        def _(dve):
            def chained(base, k, ins):
                ins.then_inc(dve_step, 1)
                dve.wait_ge(dve_step, base + k)

            def tile_of(t):
                return x_sb[:, ds(t, 1), :].rearrange("p o d -> p (o d)")

            def pair_stats(t, n, k):
                for m in range(n):
                    ins = nc.vector.bn_stats(stats[:, m, :], tile_of(t + m))
                ins.then_inc(stats_ready, 1)
                dve.wait_ge(stats_ready, k + 1)
                dve.sem_inc(dve_mark, 1)
                for m in range(n):
                    ins = nc.vector.bn_aggr(tile_moments[:, m, :], stats[:, m, :])
                ins.then_inc(moments_ready, 1)
                dve.wait_ge(moments_ready, k + 1)
                return nc.vector.tensor_copy(moments[:, ds(t, n), :], tile_moments[:, 0:n, :])

            def inverse(lo, hi):
                return nc.vector.reciprocal(moments[:, lo:hi, 1:2], moments[:, lo:hi, 1:2])

            def norm_tile(t, buf, wait=True):
                if wait:
                    dve.wait_ge(tr_ready, t - 1)
                scalars = moments[:, ds(t, 1), :].rearrange("p o a -> p (o a)")
                nc.vector.tensor_scalar(xn[:, buf, :], tile_of(t), scalars[:, 0:1], scalars[:, 1:2],
                                        ALU.subtract, ALU.mult).then_inc(xn_ready, 1)

            nc.vector.memset(x_sb[:, TILES - 1, :], 0.0).then_inc(pads_set, 1)
            nc.vector.memset(eps_col[:, :], LN_EPS).then_inc(pads_set, 1)
            nc.vector.memset(acc[:, ARENA_TILES:, :], 0.0)
            base = 0
            dve.wait_ge(ffn_loaded, 16)
            chained(base, 1, nc.vector.memset(ones, 1.0))
            k = 1
            for h in range(KH):
                chained(base, k + 1, nc.vector.tensor_single_scalar(w_sgn[:, h, :], w_raw[:, h, :], 0.0, ALU.is_lt))
                chained(base, k + 2, nc.vector.scalar_tensor_tensor(w_sgn[:, h, :], w_raw[:, h, :], 0.0, w_sgn[:, h, :], ALU.is_gt, ALU.subtract))
                chained(base, k + 3, nc.vector.scalar_tensor_tensor(mag, w_raw[:, h, :], -1.0, w_raw[:, h, :], ALU.mult, ALU.max))
                chained(base, k + 4, nc.vector.tensor_scalar(w_raw[:, h, :], mag, LOG_EPS, None, ALU.add))
                chained(base, k + 5, nc.vector.reduce_max(wmax[:, h:h + 1], w_raw[:, h, :], AX))
                chained(base, k + 6, nc.vector.reciprocal(wmax[:, 2 + h:3 + h], wmax[:, h:h + 1]))
                chained(base, k + 7, nc.vector.tensor_scalar(w_raw[:, h, :], w_raw[:, h, :], wmax[:, 2 + h:3 + h], None, ALU.mult))
                k += 7
            dve.wait_ge(ident_ready, 1)
            for h in range(KH):
                last = nc.vector.tensor_scalar(diag[:, h, :], ident[:, :], wmax[:, h:h + 1], None, ALU.mult)
            last.then_inc(w_ready, 1)
            base += k

            def group_spans():
                dve.wait_ge(dst_rows_loaded, 16 * 3)
                by_group = dst_rows[0:GROUPS // 2, :].rearrange("p (a e) -> p a e", a=2)
                nc.vector.tensor_reduce(span[0:GROUPS // 2, 0:2], by_group, axis=AX, op=ALU.min)
                nc.vector.tensor_reduce(span[0:GROUPS // 2, 2:4], by_group, axis=AX, op=ALU.max).then_inc(span_ready, 1)

            def passes_and_batches():
                def span_link(k, ins):
                    ins.then_inc(span_step, 1)
                    dve.wait_ge(span_step, k)

                dve.wait_ge(span_loaded, 16 * 2)
                dve.wait_ge(iota_ready, 1)
                dve.wait_ge(dst_ready, 1)
                nc.vector.tensor_single_scalar(dst_mod[:, :], dst_all[:, :], (P - 1) | NO_NODE, ALU.bitwise_and)
                nc.vector.tensor_copy(extra_row[:, :], greatest[0:1, :])
                nc.vector.tensor_copy(base_row[:, :], least[0:1, :])
                nc.vector.tensor_copy(least_place, least)
                span_link(1, nc.vector.tensor_tensor(narrow, greatest, least, ALU.subtract))
                nc.vector.tensor_single_scalar(extra_row[:, :], extra_row[:, :], P_SHIFT, ALU.arith_shift_right)
                nc.vector.tensor_single_scalar(base_row[:, :], base_row[:, :], P_SHIFT, ALU.arith_shift_right)
                nc.vector.tensor_single_scalar(least_place, least_place, P - 1, ALU.bitwise_and)
                span_link(2, nc.vector.tensor_single_scalar(narrow, narrow, float(P), ALU.is_lt))
                nc.vector.scalar_tensor_tensor(in_first[:, :], least_place, own_place[:, :], narrow, ALU.is_le, ALU.mult)
                nc.vector.scalar_tensor_tensor(in_second[:, :], least_place, own_place[:, :], narrow, ALU.is_gt, ALU.mult)
                span_link(3, nc.vector.tensor_tensor(extra_row[:, :], extra_row[:, :], base_row[:, :], ALU.subtract))
                span_link(4, nc.vector.tensor_single_scalar(extra_row[:, :], extra_row[:, :], 1.0, ALU.add))
                nc.vector.scalar_tensor_tensor(extra_row[:, :], narrow[0:1, :], 0.0, extra_row[:, :], ALU.is_equal, ALU.mult)
                span_link(5, nc.vector.scalar_tensor_tensor(least_by_tile, least[0:TILES, :], tile_end, group_no, ALU.is_lt, ALU.mult))
                span_link(6, nc.vector.reduce_max(need, least_by_tile, AX))
                span_link(7, nc.vector.tensor_scalar(need, need, tile_pace, float(GROUPS), ALU.max, ALU.min))
                span_link(8, nc.vector.tensor_scalar(batch_col, need, float(RING - 1), None, ALU.add))
                nc.vector.tensor_single_scalar(batch_col, batch_col, RING.bit_length() - 1, ALU.arith_shift_right).then_inc(batches_ready, 1)

            def keep_low(t, buf):
                dve.wait_ge(hi_ready, t + 1)
                nc.vector.tensor_tensor(x_lo[:, buf, :, :].rearrange("p h n -> p (h n)"), tile_of(t),
                                        x_hi[:, buf, :, :].bitcast(fp32).rearrange("p h n -> p (h n)"),
                                        ALU.subtract).then_inc(lo_ready, 1)

            def pair(i, ahead=None, first=False, stats_ahead=True):
                norm_tile(2 * i + 1, 1, wait=not first)
                keep_low(2 * i, 0)
                if stats_ahead:
                    last = pair_stats(2 * i + XC, 2, i + XC // 2)
                if ahead is not None:
                    if ahead == XCHUNKS - 1:
                        last = pair_stats(TILES - 1, 1, PAIRS)
                    last.then_inc(var_ready, 1)
                    invert_chunk(ahead)
                norm_tile(2 * i + 2, 0, wait=not first)
                keep_low(2 * i + 1, 1)

            def invert_chunk(c):
                dve.wait_ge(std_ready, c + 1)
                inverse(*chunks[c]).then_inc(inv_ready, 1)
                dve.wait_ge(inv_ready, c + 1)

            for h in range(KH):
                dve.wait_ge(w_hi_ready, h + 1)
                nc.vector.tensor_tensor(w_lo[:, h, :], wrel_sb[:, h, :], w_hi[:, h, :].bitcast(fp32),
                                        ALU.subtract).then_inc(w_lo_ready, 1)
            dve.wait_ge(x_loaded[0], 16)
            with dve.Fori(0, XC // 2 - 1) as i:
                pair_stats(2 * i, 2, i)
            pair_stats(XC - 2, 2, XC // 2 - 1).then_inc(var_ready, 1)
            invert_chunk(0)
            norm_tile(0, 0, wait=False)
            dve.wait_ge(x_loaded[1], 16)
            pair(0, first=True)
            for c in range(XCHUNKS):
                more = c + 1 < XCHUNKS
                if c > 0 and more:
                    dve.wait_ge(x_loaded[c + 1], 32 if c + 1 == XCHUNKS - 1 else 16)
                last_pair = (c + 1) * XC // 2 - 1
                if not more:
                    passes_and_batches()
                with dve.Fori(max(c * XC // 2, 1), last_pair) as i:
                    pair(i, stats_ahead=more)
                pair(last_pair, ahead=c + 1 if more else None, stats_ahead=more)
                if c == 1:
                    group_spans()
            keep_low(TILES - 1, 0)
            dve.wait_ge(rel_ready, 4 * TILES)
            nc.vector.memset(acc[:, 0:ARENA_TILES, :], 0.0).then_inc(acc_cleared, 1)
            dve.wait_ge(pool_ready, 1)

            extras = dve.alloc_register("dve_extras")
            dve.reg_mov(extras, 0)

            def make_onehot(buf, nodes, of, g):
                return nc.vector.tensor_tensor(
                    onehot[:, buf, :, :],
                    nodes.unsqueeze(1).to_broadcast([P, CH, P]),
                    of[:, ds(g * CH, CH)].unsqueeze(2).to_broadcast([P, CH, P]), ALU.is_equal)

            def onehot_by_place(buf, g):
                return make_onehot(buf, node_iota[:, 0:P], dst_mod, g)

            def onehot_in_tile(buf, tile, g):
                return make_onehot(buf, node_iota[:, ds(tile * P, P)], dst_all, g)

            def sums_of(tile):
                return acc[:, ds(tile, 1), :].rearrange("p o d -> p (o d)")

            def add_where(buf, tile, mask, g):
                return nc.vector.scalar_tensor_tensor(sums_of(tile), seg[buf], mask[:, ds(g, 1)], sums_of(tile),
                                                      ALU.mult, ALU.add)

            def base_of(g):
                return dve.value_load(base_row[0:1, ds(g, 1)], min_val=0, max_val=TILES - 1)

            def batch(layer, b):
                for i in range(RING):
                    g = b * RING + i
                    q = layer * GROUPS + g
                    onehot_by_place((i + 1) % 2, g + 1).then_inc(onehot_ready, 1)
                    first = base_of(g)
                    dve.wait_ge(seg_ready, q + 1)
                    dve.sem_inc(dve_mark, 1)
                    add_where(i % 2, first, in_first, g)
                    add_where(i % 2, first + 1, in_second, g).then_inc(acc_added, 1)
                    dve.wait_ge(acc_added, q + 1)
                    dve.sem_inc(dve_mark, 1)
                    more = dve.value_load(extra_row[0:1, ds(g, 1)], min_val=0, max_val=TILES)
                    with dve.If(more > 0):
                        with dve.Fori(0, more) as k:
                            tile = nc.s_assert_within(first + k, 0, TILES - 1, skip_runtime_bounds_check_because="the group's greatest destination lies in the last of these tiles")
                            done = dve.snap(extras, min_val=0, max_val=1 << 20)
                            onehot_in_tile(i % 2, tile, g).then_inc(onehot_extra, 1)
                            dve.wait_ge(seg_extra, done + 1)
                            dve.sem_inc(dve_mark, 1)
                            nc.vector.tensor_tensor(sums_of(tile), sums_of(tile), seg[i % 2], ALU.add).then_inc(acc_extra, 1)
                            dve.wait_ge(acc_extra, done + 1)
                            dve.reg_add(extras, extras, 1)
                    nc.vector.tensor_copy(idx_ring[:, i, :], idx_all[:, ds((g + RING) * CH, CH)]).then_inc(group_done, 1)

            onehot_by_place(0, 0).then_inc(onehot_ready, 1)
            dve.wait_ge(acc_cleared, 1)
            with dve.Fori(0, L - 1) as layer:
                dve.wait_ge(root_used, TILES * layer + 1)
                dve.sem_inc(dve_mark, 1)
                with dve.Fori(0, BATCHES) as b:
                    batch(layer, b)
            dve.wait_ge(root_used, TILES * (L - 1) + 1)
            dve.wait_ge(x_reloaded, 32)
            dve.wait_ge(biases_loaded, 32)
            with dve.Fori(0, TILES) as t:
                start = dve.value_load(batch_row[0:1, ds(t, 1)], min_val=0, max_val=BATCHES)
                end = dve.value_load(batch_row[0:1, ds(t + 1, 1)], min_val=0, max_val=BATCHES)
                with dve.If(end > start):
                    with dve.Fori(start, end) as b:
                        batch(L - 1, b)
                c = base + t * 8
                chained(c, 1, nc.vector.tensor_tensor(x1, sums_of(t), bias_bc, ALU.add))
                nc.vector.scalar_tensor_tensor(x1, x1, 0.0, tile_of(t), ALU.max, ALU.add).then_inc(x1_ready, 1)
                dve.wait_ge(x1_ready, t + 1)
                nc.vector.bn_stats(stats[:, 0, :], x1).then_inc(stats_ready, 1)
                dve.wait_ge(stats_ready, PAIRS + 2 + t)
                dve.sem_inc(dve_mark, 1)
                nc.vector.bn_aggr(moments[:, TILES, :], stats[:, 0, :]).then_inc(var_ready, 1)
                dve.wait_ge(std_ready, t + (XCHUNKS + 1))
                inverse(TILES, TILES + 1).then_inc(inv_ready, 1)
                dve.wait_ge(inv_ready, t + (XCHUNKS + 1))
                nc.vector.tensor_scalar(xn[:, 0, :], x1, moments[:, TILES, 0:1], moments[:, TILES, 1:2],
                                        ALU.subtract, ALU.mult).then_inc(z_ready, 1)
                dve.wait_ge(z_ready, t + 1)
                chained(c, 2, nc.vector.scalar_tensor_tensor(mag, xn[:, 0, :], -1.0, xn[:, 0, :], ALU.mult, ALU.max))
                chained(c, 3, nc.vector.tensor_scalar(mag, mag, LOG_EPS, None, ALU.add))
                chained(c, 4, nc.vector.reduce_max(mmax[:, 0:1], mag, AX))
                chained(c, 5, nc.vector.reciprocal(mmax[:, 1:2], mmax[:, 0:1]))
                nc.vector.tensor_scalar(mag, mag, mmax[:, 1:2], None, ALU.mult).then_inc(mag_ready, 1)
                chained(c, 6, nc.vector.tensor_tensor(x1, x1, fbias_bc, ALU.add))
                dve.wait_ge(mag_transposed, t + 1)
                nc.vector.tensor_copy(sgnT, sgn_ps).then_inc(sgnT_ready, 1)
                dve.wait_ge(lns_ready, t + 1)
                chained(c, 7, nc.vector.scalar_tensor_tensor(mag, lns_ps, mmax[:, 0:1], wmax_bc[:, :], ALU.mult, ALU.mult))
                dve.wait_ge(osgn_ready, t + 1)
                chained(c, 8, nc.vector.tensor_tensor(mag, mag, osgn, ALU.mult))
                nc.vector.tensor_tensor(tile_of(t), mag, x1, ALU.add).then_inc(out_ready, 1)
                dve.wait_ge(out_ready, t + 1)


_INS = ["x", "src", "dst", "edge_type_8", "L0_gnn_W_rel", "L0_gnn_W_root", "L0_gnn_bias", "L0_ffn_weight", "L0_ffn_bias"]
_OUTS = [((N, D), "float32")]


def kernel(**inputs):
    import numpy as _np
    import concourse.bacc as _bacc
    from concourse import mybir as _mybir
    from concourse.bass_utils import run_bass_kernel_spmd as _run

    nc = _bacc.Bacc("TRN2", target_bir_lowering=False, num_devices=1)
    arrays, args = {}, []
    for name in _INS:
        a = _np.ascontiguousarray(inputs[name])
        arrays[f"in_{name}_dram"] = a
        args.append(nc.dram_tensor(f"in_{name}_dram", a.shape, _mybir.dt.from_np(a.dtype), kind="ExternalInput").ap())
    for i, (shape, dtype) in enumerate(_OUTS):
        dt = _mybir.dt.from_np(_np.dtype(dtype))
        args.append(nc.dram_tensor(f"out_{i}_dram", shape, dt, kind="ExternalOutput").ap())
    gnn_ffn(nc, *args)
    r = _run(nc, [arrays], core_ids=[0])
    got = tuple(r.results[0][f"out_{i}_dram"] for i in range(len(_OUTS)))
    return got[0]
```
